# Optimizing a Trainium2 kernel written in Bass

```python
import numpy as np
import jax
import jax.numpy as jnp

def _softmax(x, axis=-1):
    return jax.nn.softmax(x, axis=axis)

def _gelu(x):
    return jax.nn.gelu(x, approximate=True)

def _silu(x):
    return jax.nn.silu(x)

def _sigmoid(x):
    return jax.nn.sigmoid(x)

def _layernorm(x, axis=-1, eps=1e-05):
    m = jnp.mean(x, axis=axis, keepdims=True)
    v = jnp.var(x, axis=axis, keepdims=True)
    return (x - m) / jnp.sqrt(v + eps)

def _scatter_add(tgt, idx, src, axis=0):
    return tgt.at[idx].add(src)

def _segment_sum(src, seg, n):
    return jax.ops.segment_sum(src, seg, n)
kernel_name = 'mk_perceiver_d1_seqx_r2_04012d'

def setup_inputs(seed: int=0):
    np.random.seed(seed)
    _w = jnp.asarray

    def _rec_inputs():
        import jax
        import jax.numpy as jnp
        _rk = jax.random.key(seed)
        x = 7.22e-05 + 1 * jax.random.normal(jax.random.fold_in(_rk, 1), (16, 128, 512), jnp.float32)
        _lenS = 128 - jax.random.randint(jax.random.fold_in(_rk, 7), (16,), 0, max(1, 128 // 4) + 1, jnp.int32)
        _lenS2 = 2048 - jax.random.randint(jax.random.fold_in(_rk, 8), (16,), 0, max(1, 2048 // 4) + 1, jnp.int32)
        _ctx_1024P = jax.random.normal(jax.random.fold_in(_rk, 11), (16, 16, 512), jnp.float32)
        _ctx_1024c = jax.random.dirichlet(jax.random.fold_in(_rk, 511), 0.3 * jnp.ones((16,), jnp.float32), (16, 2048))
        _ctx_1024t = jnp.einsum('bsk,bkd->bsd', _ctx_1024c, _ctx_1024P)
        _ctx_1024t = _ctx_1024t * jax.lax.rsqrt(jnp.mean(jnp.square(_ctx_1024t)) + 1e-12) * 0.953939
        ctx_1024 = 4.13588e-05 + 0.999923 * (_ctx_1024t + 0.3 * jax.random.normal(jax.random.fold_in(_rk, 611), (16, 2048, 512), jnp.float32))
        return (x, ctx_1024)
    x, ctx_1024 = _rec_inputs()

    def _L0_xattn_setup():
        import jax, jax.numpy as jnp
        import numpy as np
        EMB = 512
        NH = 16
        HD = EMB // NH
        key = jax.random.key(seed)
        ks = jax.random.split(key, 11)
        B, S = (4, 1024)
        s_in = 1.0 / np.sqrt(EMB)
        return {'q': jax.random.normal(ks[0], (B, S, EMB), jnp.float32), 'k': jax.random.normal(ks[1], (B, S, EMB), jnp.float32), 'v': jax.random.normal(ks[2], (B, S, EMB), jnp.float32), 'Wq': jax.random.normal(ks[3], (EMB, NH * HD), jnp.float32) * s_in, 'bq': jnp.zeros((NH * HD,), jnp.float32), 'Wk': jax.random.normal(ks[4], (EMB, HD), jnp.float32) * s_in, 'bk': jnp.zeros((HD,), jnp.float32), 'Wv': jax.random.normal(ks[5], (EMB, HD), jnp.float32) * s_in, 'bv': jnp.zeros((HD,), jnp.float32), 'Wo': jax.random.normal(ks[6], (NH * HD, EMB), jnp.float32) * s_in, 'bo': jnp.zeros((EMB,), jnp.float32)}
    _L0_xattn_all = _L0_xattn_setup()
    _L0_xattn_in = {k: v for k, v in _L0_xattn_all.items() if k in ('Wq', 'bq', 'Wk', 'bk', 'Wv', 'bv', 'Wo', 'bo')}
    del _L0_xattn_all

    def _L0_attn_setup():
        import jax, jax.numpy as jnp
        import numpy as np
        D_MODEL = 512
        HEAD_DIM = 128
        CHUNK = 64
        N_HEADS = D_MODEL // HEAD_DIM
        MEM_ALPHA = 0.03

        def _forward(out, Ww, Wr, decay, log_alpha):
            B, T, D = out.shape
            H, d, C = (N_HEADS, HEAD_DIM, CHUNK)
            x = out.astype(jnp.float32)
            gamma = jax.nn.sigmoid(decay)
            log_gamma = jnp.log(gamma)
            v = (x @ Ww.T).reshape(B, T, H, d).transpose(0, 2, 1, 3)
            xh = x.reshape(B, T, H, d)
            rk = xh / jnp.maximum(jnp.linalg.norm(xh, axis=-1, keepdims=True), 1e-12)
            rk = rk.transpose(0, 2, 1, 3)
            wk = jnp.concatenate([jnp.zeros((B, H, 1, d), jnp.float32), rk[:, :, :-1]], axis=2)
            BH = B * H
            gamma_bh = jnp.tile(gamma, B)
            log_gamma_bh = jnp.tile(log_gamma, B)
            v = v.reshape(BH, T, d)
            rk = rk.reshape(BH, T, d)
            wk = wk.reshape(BH, T, d)
            pad = -T % C
            if pad:
                z = ((0, 0), (0, pad), (0, 0))
                v, rk, wk = (jnp.pad(v, z), jnp.pad(rk, z), jnp.pad(wk, z))
            T_pad = T + pad
            N = T_pad // C
            v = v.reshape(BH, N, C, d)
            rk = rk.reshape(BH, N, C, d)
            wk = wk.reshape(BH, N, C, d)
            p = jnp.arange(C)
            diffs = jnp.maximum(p[:, None] - p[None, :], 0).astype(jnp.float32)
            L = jnp.tril(jnp.exp(diffs * log_gamma_bh[:, None, None]))
            strict = jnp.tril(jnp.ones((C, C), bool), -1)
            A0 = -jnp.where(strict, jnp.einsum('bnid,bnjd->bnij', wk, wk) * L[:, None], 0.0)
            eye = jnp.eye(C, dtype=jnp.float32)
            A = jnp.linalg.inv(eye - A0)
            gp = gamma_bh[:, None, None] ** p[None, :, None]
            gp_tail = gamma_bh[:, None, None] ** (C - 1 - p)[None, :, None]
            gamma_C = (gamma_bh ** C)[:, None, None]
            intra = jnp.where(strict, jnp.einsum('bnid,bnjd->bnij', rk, wk) * L[:, None], 0.0)
            rk_g = rk * gp[:, None]
            wk_g = (wk * gp_tail[:, None]).transpose(0, 1, 3, 2)

            def step(S, inp):
                A_i, v_i, wk_i, rkg_i, wkg_i, intra_i = inp
                v_corr = A_i @ v_i
                wk_corr = A_i @ wk_i
                v_new = v_corr - wk_corr @ S
                o_i = rkg_i @ S + intra_i @ v_new
                S = gamma_C * S + wkg_i @ v_new
                return (S, o_i)
            mv = lambda a: jnp.moveaxis(a, 1, 0)
            S0 = jnp.zeros((BH, d, d), jnp.float32)
            _, o = jax.lax.scan(step, S0, (mv(A), mv(v), mv(wk), mv(rk_g), mv(wk_g), mv(intra)))
            o = jnp.moveaxis(o, 0, 1).reshape(B, H, T_pad, d)
            alpha = jnp.exp(log_alpha)[None, :, None, None]
            o = (alpha * o).transpose(0, 2, 1, 3).reshape(B, T_pad, D)[:, :T]
            return out + (o @ Wr.T).astype(out.dtype)
        key = jax.random.key(seed)
        k0, k1, k2 = jax.random.split(key, 3)
        B, T = (2, 4096)
        out = jax.random.normal(k0, (B, T, D_MODEL), jnp.float32)
        Ww = jax.random.normal(k1, (D_MODEL, D_MODEL), jnp.float32) * 0.02
        Wr = jax.random.normal(k2, (D_MODEL, D_MODEL), jnp.float32) * 0.02
        decay = jnp.full((N_HEADS,), 4.6, jnp.float32)
        log_alpha = jnp.log(jnp.full((N_HEADS,), MEM_ALPHA, jnp.float32))
        return {'out': out, 'Ww': Ww, 'Wr': Wr, 'decay': decay, 'log_alpha': log_alpha}
    _L0_attn_all = _L0_attn_setup()
    _L0_attn_in = {k: v for k, v in _L0_attn_all.items() if k in ('Ww', 'Wr', 'decay', 'log_alpha')}
    del _L0_attn_all

    def _L0_ffn_setup():
        import jax, jax.numpy as jnp
        import numpy as np
        key = jax.random.key(seed)
        k1, k2, k3, k4 = jax.random.split(key, 4)
        B, T, M = (4, 1024, 512)
        E, F = (16, 2048)
        x = jax.random.normal(k1, (B, T, M), dtype=jnp.float32) * 0.02
        Wg = jax.random.normal(k2, (M, E), dtype=jnp.float32) * 0.02
        w1 = jax.random.normal(k3, (E, M, F), dtype=jnp.float32) * 0.02
        w2 = jax.random.normal(k4, (E, F, M), dtype=jnp.float32) * 0.02
        return {'x': x, 'Wg': Wg, 'w1': w1, 'w2': w2}
    _L0_ffn_all = _L0_ffn_setup()
    _L0_ffn_in = {k: v for k, v in _L0_ffn_all.items() if k in ('Wg', 'w1', 'w2')}
    del _L0_ffn_all
    return {'x': x, 'ctx_1024': ctx_1024, 'L0_xattn_Wq': _L0_xattn_in['Wq'], 'L0_xattn_bq': _L0_xattn_in['bq'], 'L0_xattn_Wk': _L0_xattn_in['Wk'], 'L0_xattn_bk': _L0_xattn_in['bk'], 'L0_xattn_Wv': _L0_xattn_in['Wv'], 'L0_xattn_bv': _L0_xattn_in['bv'], 'L0_xattn_Wo': _L0_xattn_in['Wo'], 'L0_xattn_bo': _L0_xattn_in['bo'], 'L0_attn_Ww': _L0_attn_in['Ww'], 'L0_attn_Wr': _L0_attn_in['Wr'], 'L0_attn_decay': _L0_attn_in['decay'], 'L0_attn_log_alpha': _L0_attn_in['log_alpha'], 'L0_ffn_Wg': _L0_ffn_in['Wg'], 'L0_ffn_w1': _L0_ffn_in['w1'], 'L0_ffn_w2': _L0_ffn_in['w2']}

def reference(x, ctx_1024, L0_xattn_Wq, L0_xattn_bq, L0_xattn_Wk, L0_xattn_bk, L0_xattn_Wv, L0_xattn_bv, L0_xattn_Wo, L0_xattn_bo, L0_attn_Ww, L0_attn_Wr, L0_attn_decay, L0_attn_log_alpha, L0_ffn_Wg, L0_ffn_w1, L0_ffn_w2):
    import jax
    import jax.numpy as jnp

    def _L0_xattn_ref(q, k, v, Wq, bq, Wk, bk, Wv, bv, Wo, bo):
        import jax, jax.numpy as jnp
        import numpy as np
        EMB = 512
        NH = 16
        HD = EMB // NH
        B, S, _ = q.shape
        scale = HD ** (-0.5)
        Q = (q @ Wq + bq).reshape(B, S, NH, HD).transpose(0, 2, 1, 3)
        K = k @ Wk + bk
        V = v @ Wv + bv
        scores = jnp.einsum('bhqd,bkd->bhqk', Q, K) * scale
        attn = jax.nn.softmax(scores, axis=-1)
        out = jnp.einsum('bhqk,bkd->bhqd', attn, V)
        out = out.transpose(0, 2, 1, 3).reshape(B, S, NH * HD)
        return out @ Wo + bo

    def _L0_attn_ref(out, Ww, Wr, decay, log_alpha):
        import jax, jax.numpy as jnp
        import numpy as np
        D_MODEL = 512
        HEAD_DIM = 128
        CHUNK = 64
        N_HEADS = D_MODEL // HEAD_DIM
        MEM_ALPHA = 0.03

        def _forward(out, Ww, Wr, decay, log_alpha):
            B, T, D = out.shape
            H, d, C = (N_HEADS, HEAD_DIM, CHUNK)
            x = out.astype(jnp.float32)
            gamma = jax.nn.sigmoid(decay)
            log_gamma = jnp.log(gamma)
            v = (x @ Ww.T).reshape(B, T, H, d).transpose(0, 2, 1, 3)
            xh = x.reshape(B, T, H, d)
            rk = xh / jnp.maximum(jnp.linalg.norm(xh, axis=-1, keepdims=True), 1e-12)
            rk = rk.transpose(0, 2, 1, 3)
            wk = jnp.concatenate([jnp.zeros((B, H, 1, d), jnp.float32), rk[:, :, :-1]], axis=2)
            BH = B * H
            gamma_bh = jnp.tile(gamma, B)
            log_gamma_bh = jnp.tile(log_gamma, B)
            v = v.reshape(BH, T, d)
            rk = rk.reshape(BH, T, d)
            wk = wk.reshape(BH, T, d)
            pad = -T % C
            if pad:
                z = ((0, 0), (0, pad), (0, 0))
                v, rk, wk = (jnp.pad(v, z), jnp.pad(rk, z), jnp.pad(wk, z))
            T_pad = T + pad
            N = T_pad // C
            v = v.reshape(BH, N, C, d)
            rk = rk.reshape(BH, N, C, d)
            wk = wk.reshape(BH, N, C, d)
            p = jnp.arange(C)
            diffs = jnp.maximum(p[:, None] - p[None, :], 0).astype(jnp.float32)
            L = jnp.tril(jnp.exp(diffs * log_gamma_bh[:, None, None]))
            strict = jnp.tril(jnp.ones((C, C), bool), -1)
            A0 = -jnp.where(strict, jnp.einsum('bnid,bnjd->bnij', wk, wk) * L[:, None], 0.0)
            eye = jnp.eye(C, dtype=jnp.float32)
            A = jnp.linalg.inv(eye - A0)
            gp = gamma_bh[:, None, None] ** p[None, :, None]
            gp_tail = gamma_bh[:, None, None] ** (C - 1 - p)[None, :, None]
            gamma_C = (gamma_bh ** C)[:, None, None]
            intra = jnp.where(strict, jnp.einsum('bnid,bnjd->bnij', rk, wk) * L[:, None], 0.0)
            rk_g = rk * gp[:, None]
            wk_g = (wk * gp_tail[:, None]).transpose(0, 1, 3, 2)

            def step(S, inp):
                A_i, v_i, wk_i, rkg_i, wkg_i, intra_i = inp
                v_corr = A_i @ v_i
                wk_corr = A_i @ wk_i
                v_new = v_corr - wk_corr @ S
                o_i = rkg_i @ S + intra_i @ v_new
                S = gamma_C * S + wkg_i @ v_new
                return (S, o_i)
            mv = lambda a: jnp.moveaxis(a, 1, 0)
            S0 = jnp.zeros((BH, d, d), jnp.float32)
            _, o = jax.lax.scan(step, S0, (mv(A), mv(v), mv(wk), mv(rk_g), mv(wk_g), mv(intra)))
            o = jnp.moveaxis(o, 0, 1).reshape(B, H, T_pad, d)
            alpha = jnp.exp(log_alpha)[None, :, None, None]
            o = (alpha * o).transpose(0, 2, 1, 3).reshape(B, T_pad, D)[:, :T]
            return out + (o @ Wr.T).astype(out.dtype)
        return _forward(out, Ww, Wr, decay, log_alpha)

    def _L0_ffn_ref(x, Wg, w1, w2):
        import jax, jax.numpy as jnp
        import numpy as np
        d = x.shape[-1]
        xr = x.reshape(-1, d)
        S = xr.shape[0]
        E = Wg.shape[1]
        C = (S + E - 1) // E
        gate = jax.nn.softmax(xr @ Wg, axis=-1)
        idx = jnp.argmax(gate, axis=1)
        gates_s = jnp.take_along_axis(gate, idx[:, None], axis=1)[:, 0]
        onehot = jax.nn.one_hot(idx, E, dtype=jnp.int32)
        loc = jnp.sum((jnp.cumsum(onehot, axis=0) - 1) * onehot, axis=1)
        valid = loc < C
        loc_pad = jnp.minimum(loc, C)
        dispatched = jnp.zeros((E, C + 1, d), dtype=x.dtype).at[idx, loc_pad].set(xr)
        dispatched = dispatched[:, :C]
        h = jax.nn.relu(jnp.einsum('ecm,emf->ecf', dispatched, w1))
        expert_out = jnp.einsum('ecf,efm->ecm', h, w2)
        gathered = expert_out[idx, jnp.minimum(loc, C - 1)]
        combined = gathered * (gates_s * valid.astype(x.dtype))[:, None]
        return combined.reshape(x.shape)
    x = x + _L0_xattn_ref(_layernorm(x, axis=-1), ctx_1024, ctx_1024, L0_xattn_Wq, L0_xattn_bq, L0_xattn_Wk, L0_xattn_bk, L0_xattn_Wv, L0_xattn_bv, L0_xattn_Wo, L0_xattn_bo)
    x = x + _L0_attn_ref(_layernorm(x, axis=-1), L0_attn_Ww, L0_attn_Wr, L0_attn_decay, L0_attn_log_alpha)
    x = x + _L0_ffn_ref(_layernorm(x, axis=-1), L0_ffn_Wg, L0_ffn_w1, L0_ffn_w2)
    return x

_drawn_inputs = setup_inputs


def setup_inputs(seed=0):
    import zlib

    import numpy as np

    out = dict(_drawn_inputs(seed))
    spreads = {'L0_xattn_bq': (0.0, 0.44),
     'L0_xattn_bk': (0.0, 0.8),
     'L0_xattn_bv': (0.0, 0.1),
     'L0_xattn_bo': (0.0, 0.1),
     'L0_attn_decay': (4.599999904632568, 0.6),
     'L0_attn_log_alpha': (-3.5065579414367676, 0.6)}
    factors = {'L0_attn_Ww': 8.0,
     'L0_attn_Wr': 8.0,
     'L0_ffn_Wg': 3.486,
     'L0_ffn_w1': 4.188,
     'L0_ffn_w2': 3.435}
    for name, (base, spread) in spreads.items():
        noise = np.random.default_rng([zlib.crc32(name.encode()), seed]).standard_normal(out[name].shape)
        drawn = base * np.exp(spread * noise) if base else spread * noise
        out[name] = jnp.asarray(drawn.astype(out[name].dtype))
    for name, factor in factors.items():
        out[name] = (out[name] * factor).astype(out[name].dtype)
    return out
```

```python
from contextlib import ExitStack

import numpy as np
import concourse.bass as bass
from concourse import mybir

F32, F32R, U32 = mybir.dt.float32, mybir.dt.float32r, mybir.dt.uint32
ALU, ACT, AX = mybir.AluOpType, mybir.ActivationFunctionType, mybir.AxisListType

P = 128
B, S, D = 16, 2048, 512
NH, HD = 16, 32
DC = D // P
KB = S // P
HG = NH // 4
DH = 4
CH = 64
E, F = 16, 2048
FT = F // P
CAP = (B * P + E - 1) // E
ROWS = E * CAP
EPS = 1e-5
SCALE = float(HD) ** -0.5
C_IDENT, C_EXPO, C_EXPO_I, C_UPPER, C_PAIR, C_PAIR_T, C_ONES, C_DUMP, C_LEVEL = range(9)
NCONST = C_LEVEL + 6
UNITS = HG * KB


class Lane:

    def __init__(self, sem):
        self.sem, self.per, self.n = sem, None, 0


class Stage:

    def __init__(self, name, lanes, events, clock=0.0):
        self.name, self.lanes, self.events, self.t, self.steps = name, lanes, events, clock, []

    def at(self, t):
        assert t >= self.t - 1e-9, (self.name, self.t, t)
        self.t = t

    def step(self, eng, fn, name=None, after=(), lane=None, by=1):
        if lane is None:
            lane = self.lanes[(self.name, eng)]
        if name is not None:
            lane.n += by
            assert name not in self.events, name
            self.events[name] = (lane, lane.n)
        self.steps.append((self.t, eng, fn, name is not None and (lane, by), tuple(after)))

    def dma(self, eng, fn, name, lane, after=()):
        self.step(eng, fn, name, after, lane, 16)


def issue(e, eng, parts, events, bases=None):
    merged = sorted(((s[0], n, j, s, b) for n, (st, b) in enumerate(parts)
                     for j, s in enumerate(st.steps)), key=lambda m: m[:3])
    for _, _, _, (_, on, fn, mark, after), b in merged:
        if on != eng:
            continue
        need = {}
        for a in after:
            name, ago = a if isinstance(a, tuple) else (a, 0)
            lane, k = events[name]
            if not isinstance(b, int) or b >= ago:
                off = b if isinstance(b, int) else b[1]
                need[lane] = max(need.get(lane, -10**6), (off - ago) * lane.per + k)
        for lane, n in need.items():
            if not isinstance(b, int):
                if lane not in bases:
                    bases[lane] = e.snap(b[0] * lane.per)
                n = bases[lane] + n
            e.wait_ge(lane.sem, n)
        ins = fn(e, b if isinstance(b, int) else b[0] + b[1])
        if mark:
            ins.then_inc(mark[0].sem, mark[1])


def first_pipeline(nc, T, keep):
    with ExitStack() as ctx:
        def sb(name, shape, dt=F32):
            return ctx.enter_context(nc.sbuf_tensor(name, shape, dt))

        def lane(name):
            return Lane(ctx.enter_context(nc.semaphore(name)))

        bank = [ctx.enter_context(nc.psum_tensor(f"bank{i}", [P, 512], F32)) for i in range(8)]
        A_BANK, B_BANK, PV_BANK, T_BANK, KV_BANK, POST = bank[0:2], bank[2:4], bank[4], bank[5], bank[6], bank[7]

        cst = sb("cst", [P, NCONST, P])
        ident = cst[:, C_IDENT, :]
        iota = sb("iota", [P, E])
        wq, wo, ww, wr = (sb(n, [P, DC, D]) for n in ("wq", "wo", "ww", "wr"))
        wkv = sb("wkv", [P, DC, 2 * HD])
        wg = sb("wg", [P, DC, E])
        bq, bo, bkv = sb("bq", [P, D]), sb("bo", [P, D]), sb("bkv", [P, 2 * HD])
        decay, lalpha = sb("decay", [P, DH]), sb("lalpha", [P, DH])
        logg, alpha, gamma = sb("logg", [P, DH]), sb("alpha", [P, DH]), sb("gamma", [P, DH])
        decT, decI, dec1, dec1T = (sb(n, [P, DH, P]) for n in ("decT", "decI", "dec1", "dec1T"))
        mhalf, eps = sb("mhalf", [P, DH]), sb("eps", [P, 1])
        pad_dve, pad_pool = sb("pad_dve", [P, 1]), sb("pad_pool", [P, 1])
        cx = [sb(f"cx{c}", [P, 4, D]) for c in range(4)]
        cxT = [sb(f"cxT{i}", [P, DC, P]) for i in range(2)]
        kv = [sb(f"kv{i}", [P, KB, 2 * HD + 1]) for i in range(2)]
        k3 = [sb(f"k3{i}", [P, 4, 3 * HD]) for i in range(2)]
        kT = [sb(f"kT{i}", [P, S], F32R) for i in range(2)]
        qT = [sb(f"qT{i}", [P, NH * P], F32R) for i in range(2)]
        xin, xn, xnT, qf = sb("xin", [P, D]), sb("xn", [P, D]), sb("xnT", [P, DC, P]), sb("qf", [P, D])
        q3 = sb("q3", [P, NH, 3 * HD])
        st1, mv1, rs1 = sb("st1", [P, 6]), sb("mv1", [P, 2]), sb("rs1", [P, 2])
        pr = [sb(f"pr{i}", [P, 512]) for i in range(3)]
        mpart = [sb(f"mpart{i}", [P, 16]) for i in range(2)]
        mneg = sb("mneg", [P, 4])
        mrow = [sb(f"mrow{i}", [4, P], F32R) for i in range(2)]
        rsum = sb("rsum", [P, 4])
        att = [sb(f"att{i}", [P, D]) for i in range(2)]
        (xr, oT1, x1, xn2, x12, rk, xn2T, V, MT, IT, X, XT, Y, Vn, oT2, x2, xn3, xn3T) = (
            sb(n, [P, D]) for n in ("xr", "oT1", "x1", "xn2", "x12", "rk", "xn2T", "V", "MT", "IT", "X", "XT",
                                    "Y", "Vn", "oT2", "x2", "xn3", "xn3T"))
        rkT = sb("rkT", [P, DH, P + 1])
        st2, mv2, rs2 = sb("st2", [P, 6]), sb("mv2", [P, 2]), sb("rs2", [P, 2])
        st3, mv3, rs3 = sb("st3", [P, 6]), sb("mv3", [P, 2]), sb("rs3", [P, 2])
        ss, rn = sb("ss", [P, DH]), sb("rn", [P, DH])
        lg, eg, oh, oh2 = (sb(n, [P, E]) for n in ("lg", "eg", "oh", "oh2"))
        before = sb("before", [P, E])
        sc = sb("sc", [P, 12])
        sidx = sb("sidx", [P, 1], U32)
        gidx_all, gate_all = keep

        lanes = {(s, e): lane(f"{s}_{e}") for s in ("prep", "attn", "max", "post") for e in ("pe", "dve", "act", "pool")}
        L_ctx = [lane(f"ctx_in{c}") for c in range(4)]
        L_x, L_xr, L_x2, L_scat = lane("x_in"), lane("xr_in"), lane("x2_out"), lane("scatter_out")
        L_mrow = [lane(f"mrow_dma{g}") for g in range(HG)]
        ev = {}

        def aggregate(e, out, in_):
            e.memset(pad_dve[:], 0.0)
            return e.bn_aggr(out, in_)

        def scatter(e):
            e.tensor_tensor(pad_pool[:], mhalf[:, 0:1], mhalf[:, 0:1], ALU.mult)
            return e.indirect_dma_start(
                out=T["disp"][:], out_offset=bass.IndirectOffsetOnAxis(ap=sidx[:, 0:1], axis=0), in_=xn3[:],
                in_offset=None)

        def transposes(e, out, src, n=4, m=P):
            for j in range(n):
                i = e.transpose(out[0:m, j * P:(j + 1) * P], src(j), ident)
            return i

        def copy(on, e, out, in_):
            return e.copy(out, in_) if on == "act" else e.tensor_copy(out, in_)

        load = Stage("load", lanes, ev)
        for c in range(4):
            load.at(8.0 * c + 19.5)
            load.dma("sp", lambda e, b, c=c: e.dma_start(cx[c][:], T["ctx"][bass.ds(b, 1)].rearrange(
                "o (p c k) d -> c p (o k) d", c=4, k=4)[c]), f"ctx{c}", L_ctx[c],
                after=[(f"T{4 * c + 3}", 1)])

        def prep_steps(st, q):
            st.at(0.0)
            st.dma("sp", lambda e, b: e.dma_start(xin[:], T["x"][bass.ds(b, 1)].rearrange("o p d -> p (o d)")),
                   "x", L_x, after=[("xn", 1)])
            st.at(2.0)
            st.step("dve", lambda e, b: e.bn_stats(st1[:], xin[:]), "st1", ["x"])
            st.step("dve", lambda e, b: aggregate(e, mv1[:], st1[:]), "mv1", ["st1"])
            st.step("pool", lambda e, b: e.tensor_tensor(rs1[:, 0:1], mv1[:, 1:2], eps[:, 0:1], ALU.add), "ve1", ["mv1"])
            st.step("pool", lambda e, b: e.tensor_tensor(rs1[:, 1:2], rs1[:, 0:1], mhalf[:, 0:1], ALU.pow), "rs1",
                    ["ve1"])
            st.at(3.5)
            st.step("dve", lambda e, b: e.tensor_scalar(xn[:], xin[:], mv1[:, 0:1], rs1[:, 1:2], ALU.subtract,
                                                        ALU.mult), "xn", ["mv1", "rs1", ("xnTp", 1)])
            st.at(4.5)
            st.step("pe", lambda e, b: transposes(e, T_BANK, lambda j: xn[:, j * P:(j + 1) * P]), "xnTp",
                    ["xn", ("kTc3", 1)])
            st.at(5.0)
            st.step("act", lambda e, b: e.copy(xnT[:].rearrange("p c t -> p (c t)"), T_BANK[:]), "xnT",
                    ["xnTp"])

            def q_proj(e, b):
                for c in range(DC):
                    i = e.matmul(KV_BANK[:], xnT[:, c, :], wq[:, c, :], start=c == 0, stop=c == DC - 1)
                return i
            st.at(6.5)
            st.step("pe", q_proj, "Qp", ["xnT", ("kv3", 1)])
            st.at(7.0)
            st.step("dve", lambda e, b: e.scalar_tensor_tensor(qf[:], KV_BANK[:], SCALE, bq[:], ALU.mult, ALU.add),
                    "qf", ["Qp", ("qh", 1)])
            q4, qf4 = q3[:], qf[:].rearrange("p (h d) -> p h d", h=NH)
            qh = q4.bitcast(F32R)
            st.step("dve", lambda e, b: e.tensor_copy(qh[:, :, 0:HD], qf4), "qh0", ["qf", ("qTp3", 1)])
            st.step("act", lambda e, b: e.copy(qh[:, :, HD:2 * HD], qf4), "qh", ["qf", ("qTp3", 1)])
            st.step("dve", lambda e, b: e.tensor_tensor(q4[:, :, 2 * HD:3 * HD], qf4, q4[:, :, 0:HD], ALU.subtract),
                    "ql", ["qh0"])
            for g in range(HG):
                st.at(9.0 + g)
                st.step("pe", lambda e, b, g=g: transposes(e, T_BANK, lambda j: q3[:, 4 * g + j, :], 4, 3 * HD),
                        f"qTp{g}", ["qh", "ql", "xnT" if g == 0 else f"qT{g - 1}"])
                st.at(9.3 + g)
                on = "act" if g % 2 else "dve"
                st.step(on, lambda e, b, g=g, on=on: copy(on, e, qT[q][0:3 * HD, g * 512:(g + 1) * 512], T_BANK[0:3 * HD, :]),
                        f"qT{g}", [f"qTp{g}", (f"B{UNITS - 1}", 2)])
            for k in range(KB):
                t = 13.0 + 2.0 * k
                c, kk = divmod(k, 4)
                st.at(t)
                prev = "qT3" if k == 0 else (f"kTc{k // 4 - 1}" if k % 4 == 0 and k else f"cxT{k - 1}")
                st.step("pe", lambda e, b, c=c, kk=kk: transposes(
                    e, T_BANK, lambda j: cx[c][:, kk, j * P:(j + 1) * P]), f"T{k}", [f"ctx{c}", prev])
                st.at(t + 0.2)
                on = "act" if k % 2 else "dve"
                st.step(on, lambda e, b, k=k, on=on: copy(
                    on, e, cxT[k % 2][:].rearrange("p c t -> p (c t)"), T_BANK[:]), f"cxT{k}",
                    [f"T{k}"] + ([f"KVp{k - 2}"] if k > 1 else [(f"KVp{KB - 2 + k}", 1)]))

                def kv_proj(e, b, k=k, kk=kk):
                    o = KV_BANK[:, 64 * kk:64 * kk + 64]
                    for j in range(DC):
                        i = e.matmul(o, cxT[k % 2][:, j, :], wkv[:, j, :], start=j == 0, stop=j == DC - 1)
                    return i
                st.at(t + 1.2)
                st.step("pe", kv_proj, f"KVp{k}", [f"cxT{k}"] + (
                    (["qf"] if k == 0 else [f"kv{c - 1}"]) if kk == 0 else []))
                if kk == 3:
                    r = slice(4 * c, 4 * c + 4)
                    ph = c % 2
                    st.step("dve", lambda e, b, r=r: e.tensor_tensor(
                        kv[q][:, r, 0:2 * HD], KV_BANK[:, 0:256].rearrange("p (k n) -> p k n", k=4),
                        bkv[:].unsqueeze(1).to_broadcast([P, 4, 2 * HD]), ALU.add), f"kv{c}",
                        [f"KVp{k}", (f"PV{UNITS - 1}", 2)])
                    kr = k3[ph][:].bitcast(F32R)
                    w = [f"kTp{c - 2}"] if c > 1 else [(f"kTp{c + 2}", 1)]
                    st.step("act", lambda e, b, r=r, kr=kr: e.copy(kr[:, :, 0:HD], kv[q][:, r, 0:HD]),
                            f"kh0{c}", [f"kv{c}"] + w)
                    st.step("dve", lambda e, b, r=r, kr=kr: e.tensor_copy(kr[:, :, 2 * HD:3 * HD], kv[q][:, r, 0:HD]),
                            f"kh1{c}", [f"kv{c}"] + w)
                    st.step("pool", lambda e, b, r=r, ph=ph: e.tensor_tensor(
                        k3[ph][:, :, HD:2 * HD], kv[q][:, r, 0:HD], k3[ph][:, :, 0:HD], ALU.subtract),
                        f"kl{c}", [f"kh0{c}"])
                    st.at(t + 1.8)
                    st.step("pe", lambda e, b, ph=ph: transposes(e, T_BANK, lambda j: k3[ph][:, j, :], 4, 3 * HD),
                            f"kTp{c}", [f"kh1{c}", f"kl{c}", f"cxT{k}"])
                    st.step("dve", lambda e, b, c=c: e.tensor_copy(kT[q][0:3 * HD, c * 512:(c + 1) * 512],
                                                                   T_BANK[0:3 * HD, :]), f"kTc{c}",
                            [f"kTp{c}", (f"B{UNITS - 1}", 2)])
            maxima(st, 0, q, 47.5)

        def maxima(st, g, q, t0):
            for n in range(17):
                use = 17 * g + n
                a = A_BANK[use % 2]
                prev = 17 * g + n - 2
                w = [f"A_free{prev}"] if prev >= 0 else [(f"A_free{prev + 17 * HG}", 1)]
                if n < 16:
                    h, c = divmod(n, 4)
                    st.at(t0 + 0.7 * n)
                    st.step("pe", lambda e, b, h=h, c=c, a=a: e.matmul(
                        a[:], qT[q][0:3 * HD, (4 * g + h) * P:(4 * g + h + 1) * P],
                        kT[q][0:3 * HD, c * 512:(c + 1) * 512], start=True, stop=True), f"A{use}",
                        w + ([f"qT{g}", "kTc3", "qT3"] if n == 0 else []))
                    st.at(t0 + 0.7 * n + 0.3)
                    st.step("dve", lambda e, b, n=n, a=a: e.tensor_reduce(mpart[g % 2][:, n:n + 1], a[:], AX.X,
                                                                          ALU.max), f"A_free{use}", [f"A{use}"])
                else:
                    st.step("dve", lambda e, b: e.tensor_reduce(
                        mneg[:], mpart[g % 2][:].rearrange("p (h c) -> p h c", h=4), AX.X, ALU.max, negate=True),
                        f"mneg{g}", [f"A_free{use - 1}", (f"A{17 * g - 1}", 0) if g else (f"A{17 * HG - 1}", 1)])
                    st.at(t0 + 0.7 * n + 0.8)
                    st.step("pe", lambda e, b, a=a: e.transpose(a[0:4, 0:P], mneg[:], ident), f"A{use}",
                            w + [f"mneg{g}"])
                    st.at(t0 + 0.7 * n + 1.0)
                    st.step("act", lambda e, b, a=a: e.copy(mrow[g % 2][:], a[0:4, 0:P]), f"A_free{use}",
                            [f"A{use}", (f"mrow{g - 2}", 0) if g > 1 else (f"mrow{g + 2}", 1)])
                    st.dma("sp", lambda e, b: e.dma_start(
                        qT[q][3 * HD:3 * HD + 1, g * 512:(g + 1) * 512].bitcast(F32).rearrange(
                            "o (h t) -> o h t", h=4), mrow[g % 2][:].bitcast(F32)), f"mrow{g}", L_mrow[g], after=[f"A_free{use}"])

        def attn_steps(st, q):
            mine = []
            for g in range(HG):
                for k in range(KB):
                    u = g * KB + k

                    def scores(st=st, g=g, k=k, u=u):
                        w = [f"exp{u - 2}"] if u > 1 else [(f"exp{u - 2 + UNITS}", 1)]
                        if k == 0:
                            w += [f"mrow{g}"]
                        st.step("pe", lambda e, b: e.matmul(
                            B_BANK[u % 2][:], kT[q][0:3 * HD + 1, k * P:(k + 1) * P],
                            qT[q][0:3 * HD + 1, g * 512:(g + 1) * 512], start=True, stop=True), f"B{u}", w)
                    mine.append((u, scores))

                    def expo(st=st, g=g, k=k, u=u):
                        st.step("act", lambda e, b: e.activation(pr[u % 3][:], B_BANK[u % 2][:], ACT.Exp),
                                f"exp{u}", [f"B{u}", f"PV{u - 3}" if u > 2 else (f"PV{u - 3 + UNITS}", 1)])
                    mine.append((u + 0.1, expo))

                    def weigh(st=st, g=g, k=k, u=u):
                        def f(e, b):
                            for j in range(4):
                                i = e.matmul(PV_BANK[:, 33 * j:33 * j + 33], pr[u % 3][:, j * P:(j + 1) * P],
                                             kv[q][:, k, HD:2 * HD + 1], start=k == 0 and j == 0,
                                             stop=k == KB - 1, skip_group_check=True)
                            return i
                        w = [f"exp{u}"]
                        if k == 0:
                            w += [f"att{g - 1}" if g else (f"att{HG - 1}", 1), "kv3"]
                        st.step("pe", f, f"PV{u}", w)
                    mine.append((u + 1.2, weigh))

                def normalise(st=st, g=g):
                    o = PV_BANK[:, 0:132].rearrange("p (h n) -> p h n", h=4)
                    st.step("dve", lambda e, b: e.reciprocal(rsum[:], o[:, :, HD]), f"rsum{g}",
                            [f"PV{g * KB + KB - 1}"])
                    st.step("dve", lambda e, b: e.tensor_tensor(
                        att[q][:, g * P:(g + 1) * P].rearrange("p (h n) -> p h n", h=4), o[:, :, 0:HD],
                        rsum[:].unsqueeze(2).to_broadcast([P, 4, HD]), ALU.mult), f"att{g}",
                        [f"rsum{g}", ("oT1p", 2)])
                mine.append((g * KB + KB + 0.6, normalise))
            for t, f in sorted(mine, key=lambda m: m[0]):
                st.at(t)
                f()

        def heads(ap, n=DH):
            return ap.rearrange("p (h t) -> p h t", h=n)

        def post_steps(st, q):
            hop = [2.2]

            def pe(fn, name, after=()):
                st.at(hop[0])
                st.step("pe", fn, name, list(after))
                hop[0] += 0.45

            def then(eng, fn, name, after=()):
                st.at(max(st.t, hop[0]))
                st.step(eng, fn, name, list(after))

            def gap(n=0.85):
                hop[0] = max(hop[0], st.t) + n

            def norm(src, dst, stt, mv, rs, tag, dep, war):
                then("dve", lambda e, b: e.bn_stats(stt[:], src[:]), "st" + tag, [dep])
                then("dve", lambda e, b: aggregate(e, mv[:], stt[:]), "mv" + tag, ["st" + tag])
                then("pool", lambda e, b: e.tensor_tensor(rs[:, 0:1], mv[:, 1:2], eps[:, 0:1], ALU.add), "ve" + tag,
                     ["mv" + tag])
                then("pool", lambda e, b: e.tensor_tensor(rs[:, 1:2], rs[:, 0:1], mhalf[:, 0:1], ALU.pow),
                     "rs" + tag, ["ve" + tag])
                gap(0.6)
                then("dve", lambda e, b: e.tensor_scalar(dst[:], src[:], mv[:, 0:1], rs[:, 1:2], ALU.subtract,
                                                         ALU.mult), "xn" + tag, ["mv" + tag, "rs" + tag] + war)
                gap(0.6)

            def project(name, lhs, w, after):
                def f(e, b):
                    for c in range(DC):
                        i = e.matmul(POST[:], lhs[:, c * P:(c + 1) * P], w[:, c, :], start=c == 0, stop=c == DC - 1)
                    return i
                pe(f, name, after)

            def per_head(name, lhs, rhs, after):
                def f(e, b):
                    for h in range(DH):
                        i = e.matmul(POST[:, h * P:(h + 1) * P], lhs(h), rhs(h), start=True, stop=True)
                    return i
                pe(f, name, after)

            def cut(t):
                return lambda h: t[:, h * P:(h + 1) * P]

            st.at(0.0)
            st.dma("sp", lambda e, b: e.dma_start(xr[:], T["x"][bass.ds(b, 1)].rearrange("o p d -> p (o d)")),
                   "xr", L_xr, after=[("x1", 1)])
            st.at(2.0)
            st.step("pool", lambda e, b: e.tensor_tensor(xr[:], xr[:], bo[:], ALU.add), "xb", ["xr"])
            pe(lambda e, b: transposes(e, POST, cut(att[q])), "oT1p", ["att3", ("lg", 1)])
            then("act", lambda e, b: e.copy(oT1[:], POST[:]), "oT1", ["oT1p"])
            gap()
            project("x1p", oT1, wo, ["oT1"])
            then("dve", lambda e, b: e.tensor_tensor(x1[:], POST[:], xr[:], ALU.add), "x1", ["x1p", "xb"])
            norm(x1, xn2, st2, mv2, rs2, "2", "x1", [])
            then("pool", lambda e, b: e.tensor_tensor(x12[:], x1[:], xn2[:], ALU.add), "x12", ["xn2"])
            pe(lambda e, b: transposes(e, POST, cut(xn2)), "xn2Tp", ["xn2"])
            then("act", lambda e, b: e.copy(xn2T[:], POST[:]), "xn2T", ["xn2Tp"])
            then("dve", lambda e, b: e.tensor_tensor(rk[:], xn2[:], xn2[:], ALU.mult), "sq", ["xn2"])
            then("dve", lambda e, b: e.tensor_reduce(ss[:], heads(rk[:]), AX.X, ALU.add), "ss", ["sq"])
            then("dve", lambda e, b: e.tensor_scalar(rn[:], ss[:], 1e-24, None, ALU.max), "ssm", ["ss"])
            then("pool", lambda e, b: e.tensor_tensor(rn[:], rn[:], mhalf[:], ALU.pow), "rn", ["ssm"])
            gap(0.5)
            then("dve", lambda e, b: e.tensor_tensor(heads(rk[:]), heads(xn2[:]),
                                                     rn[:].unsqueeze(2).to_broadcast([P, DH, P]), ALU.mult),
                 "rk", ["rn", "ss"])
            gap(0.3)
            project("Vp", xn2T, ww, ["xn2T"])
            then("act", lambda e, b: e.copy(V[:], POST[:]), "V", ["Vp"])
            gap()
            pe(lambda e, b: transposes(e, POST, cut(rk)), "rkTp", ["rk", "V"])
            then("act", lambda e, b: e.copy(rkT[:, :, 1:P + 1], heads(POST[:])), "rkT", ["rkTp"])
            gap()
            per_head("Gp", lambda h: rkT[:, h, 0:P], lambda h: rkT[:, h, 0:P], ["rkT"])
            then("dve", lambda e, b: e.tensor_tensor(MT[:], POST[:], decT[:].rearrange("p h t -> p (h t)"),
                                                     ALU.mult), "MT", ["Gp"])
            then("dve", lambda e, b: e.tensor_tensor(X[:], POST[:], dec1[:].rearrange("p h t -> p (h t)"),
                                                     ALU.mult), "X1a", ["Gp"])
            then("dve", lambda e, b: e.tensor_tensor(XT[:], POST[:], dec1T[:].rearrange("p h t -> p (h t)"),
                                                     ALU.mult), "XT1a", ["Gp"])
            idb = ident.unsqueeze(1).to_broadcast([P, DH, P])
            then("pool", lambda e, b: e.tensor_tensor(heads(X[:]), heads(X[:]), idb, ALU.add), "X1", ["X1a"])
            then("pool", lambda e, b: e.tensor_tensor(heads(XT[:]), heads(XT[:]), idb, ALU.add), "XT1", ["XT1a"])
            gap(1.4)
            per_head("Ip", lambda h: rkT[:, h, 0:P], lambda h: rkT[:, h, 1:P + 1], ["XT1a"])
            then("dve", lambda e, b: e.tensor_tensor(IT[:], POST[:], decI[:].rearrange("p h t -> p (h t)"),
                                                     ALU.mult), "IT", ["Ip"])
            gap()
            xs, xts, last = "X1", "XT1", "IT"
            for lv in range(6):
                s = 2 << lv
                per_head(f"Yp{s}", cut(MT), cut(X), ["MT", xs, last])
                then("dve", lambda e, b, lv=lv: e.tensor_tensor(
                    heads(Y[:]), heads(POST[:]), cst[:, C_LEVEL + lv, :].unsqueeze(1).to_broadcast([P, DH, P]),
                    ALU.mult), f"Y{s}", [f"Yp{s}"])
                gap()
                if s < CH:
                    per_head(f"Zp{s}", cut(XT), cut(Y), [f"Y{s}", xts])
                    then("dve", lambda e, b: e.tensor_tensor(X[:], X[:], POST[:], ALU.subtract), f"X{s}",
                         [f"Zp{s}"])
                    gap()
                per_head(f"ZTp{s}", cut(Y), cut(XT), [f"Y{s}", xts] + ([f"X{s}"] if s < CH else []))
                then("dve", lambda e, b: e.tensor_tensor(XT[:], XT[:], POST[:], ALU.subtract), f"XT{s}",
                     [f"ZTp{s}"])
                gap()
                xs, xts, last = f"X{s}", f"XT{s}", f"XT{s}"
            per_head("Vnp", cut(XT), cut(V), ["XT64"])
            then("act", lambda e, b: e.copy(Vn[:], POST[:]), "Vn", ["Vnp"])
            gap()
            per_head("oT2p", cut(Vn), cut(IT), ["Vn"])
            then("act", lambda e, b: e.copy(oT2[:], POST[:]), "oT2", ["oT2p"])
            gap()
            project("x2p", oT2, wr, ["oT2"])
            then("dve", lambda e, b: e.tensor_tensor(x2[:], POST[:], x12[:], ALU.add), "x2",
                 ["x2p", "x12", ("x2out", 1)])
            st.dma("sp", lambda e, b: e.dma_start(T["x2"][bass.ds(b, 1)].rearrange("o p d -> p (o d)"), x2[:]),
                   "x2out", L_x2, after=["x2"])
            norm(x2, xn3, st3, mv3, rs3, "3", "x2", [("scat", 1)])
            pe(lambda e, b: transposes(e, POST, cut(xn3)), "xn3Tp", ["xn3"])
            then("act", lambda e, b: e.copy(xn3T[:], POST[:]), "xn3T", ["xn3Tp"])
            gap()

            def logits(e, b):
                for c in range(DC):
                    i = e.matmul(POST[:, 0:E], xn3T[:, c * P:(c + 1) * P], wg[:, c, :], start=c == 0,
                                 stop=c == DC - 1)
                return i
            pe(logits, "lgp", ["xn3T"])
            then("dve", lambda e, b: e.tensor_copy(lg[:], POST[:, 0:E]), "lg0", ["lgp"])
            then("dve", lambda e, b: e.tensor_reduce(sc[:, 0:1], lg[:], AX.X, ALU.max, negate=True), "lmax",
                 ["lg0", ("eg", 1)])
            then("act", lambda e, b: e.activation(eg[:], lg[:], ACT.Exp, bias=sc[:, 0:1],
                                                  accum_out=sc[:, 1:2]), "eg", ["lmax", ("gate", 1)])
            then("dve", lambda e, b: e.tensor_reduce(sc[:, 2:3], eg[:], AX.X, ALU.max), "emax", ["eg"])
            then("dve", lambda e, b: e.scalar_tensor_tensor(oh2[:], eg[:], sc[:, 2:3], iota[:], ALU.is_ge, ALU.mult),
                 "cand", ["emax"])
            then("dve", lambda e, b: e.tensor_reduce(sc[:, 3:4], oh2[:], AX.X, ALU.min), "best", ["cand"])
            then("dve", lambda e, b: e.tensor_scalar(oh[:], iota[:], sc[:, 3:4], None, ALU.is_equal), "oh",
                 ["best"])
            gap(0.6)

            def places(e, b):
                e.matmul(POST[:, 0:E], cst[:, C_UPPER, :], oh[:], start=True, stop=False)
                return e.matmul(POST[:, 0:E], cst[:, C_ONES, :], before[:], start=False, stop=True)
            pe(places, "locp", ["oh", "lg0", ("before", 1)])
            then("dve", lambda e, b: e.tensor_tensor(oh2[:], POST[:, 0:E], oh[:], ALU.mult), "lg", ["locp"])
            then("dve", lambda e, b: e.tensor_tensor(before[:], before[:], oh[:], ALU.add), "before", ["locp"])
            then("dve", lambda e, b: e.tensor_reduce(sc[:, 4:5], oh2[:], AX.X, ALU.add), "loc", ["lg"])
            then("dve", lambda e, b: e.tensor_scalar(sc[:, 5:6], sc[:, 4:5], float(CAP), None, ALU.is_lt), "valid",
                 ["loc"])
            then("dve", lambda e, b: e.tensor_scalar(sc[:, 6:7], sc[:, 4:5], float(CAP - 1), None, ALU.min), "locc",
                 ["loc"])
            then("dve", lambda e, b: e.tensor_scalar(sc[:, 7:8], sc[:, 3:4], float(CAP), float(E * CAP), ALU.mult,
                                                     ALU.add), "row0", ["best"])
            then("dve", lambda e, b: e.tensor_tensor(sc[:, 8:9], sc[:, 7:8], sc[:, 6:7], ALU.add), "row",
                 ["row0", "locc"])
            then("dve", lambda e, b: e.tensor_tensor(sc[:, 9:10], sc[:, 8:9], cst[:, C_DUMP, 0:1], ALU.subtract),
                 "d0", ["row"])
            then("dve", lambda e, b: e.scalar_tensor_tensor(sc[:, 10:11], sc[:, 9:10], sc[:, 5:6],
                                                            cst[:, C_DUMP, 0:1], ALU.mult, ALU.add), "d1",
                 ["d0", "valid"])
            then("dve", lambda e, b: e.tensor_copy(sidx[:], sc[:, 10:11]), "sidx", ["d1", ("scat", 1)])
            then("dve", lambda e, b: e.tensor_copy(gidx_all[:, bass.ds(b, 1)], sc[:, 8:9]), "gidx", ["row"])
            then("dve", lambda e, b: e.reciprocal(sc[:, 11:12], sc[:, 1:2]), "ginv", ["eg"])
            then("dve", lambda e, b: e.tensor_tensor(gate_all[:, bass.ds(b, 1)], sc[:, 11:12], sc[:, 5:6],
                                                     ALU.mult), "gate", ["ginv", "valid"])
            st.dma("pool", lambda e, b: scatter(e), "scat", L_scat, after=["sidx", "xn3"])

        pre, att_st, post = {}, {}, {}
        all_lanes = list(lanes.values()) + L_ctx + [L_x, L_xr, L_x2, L_scat] + L_mrow
        for q in (0, 1):
            names = ev if q == 0 else {}
            keep_n = [l.n for l in all_lanes]
            if q:
                for l in [l for l in all_lanes if l not in L_ctx]:
                    l.n = 0
            pre[q], post[q] = Stage("prep", lanes, names), Stage("post", lanes, names)
            prep_steps(pre[q], q)
            am, mx = Stage("attn", lanes, names), Stage("max", lanes, names)
            attn_steps(am, q)
            att_st[q] = [am, mx]
            for g in range(1, HG):
                maxima(mx, g, q, 16.0 * (g - 1) + 0.5)
            post_steps(post[q], q)
            if q:
                assert keep_n == [l.n for l in all_lanes]
        for l in all_lanes:
            l.per = l.n

        def parts(i, known):
            out = []
            for off, sts in ((2, lambda q: [load]), (1, lambda q: [pre[q]]), (0, lambda q: att_st[q]),
                             (-1, lambda q: [post[q]])):
                if known is not None:
                    b = known + off
                    if not 0 <= b < B:
                        continue
                    out += [(s, b) for s in sts(b % 2)]
                else:
                    reg, d = i
                    out += [(s, (reg, d + off)) for s in sts((d + off) % 2)]
            return out

        s_w, s_c, s_setup, s_zero = (ctx.enter_context(nc.semaphore(n)) for n in
                                     ("w_in", "const_in", "setup_dve", "zero_out"))
        s_sp = ctx.enter_context(nc.semaphore("setup_pool"))
        s_sa = ctx.enter_context(nc.semaphore("setup_act"))
        N_W, SETUP = 11, 2 + 4 * DH + 3

        def run(e, eng):
            for i in (-2, -1, 0, 1):
                issue(e, eng, parts(None, i), ev)
            with e.Fori(2, B - 3, 2) as r:
                bases = {}
                for d in (0, 1):
                    issue(e, eng, parts((r, d), None), ev, bases)
            for i in (B - 2, B - 1, B):
                issue(e, eng, parts(None, i), ev)

        block = ctx.enter_context(nc.Block())

        @block.sync
        def _(e):
            e.dma_start(cst[:], T["consts"]).then_inc(s_c, 16)
            for dst, src in ((iota[:], T["iota"]), (decay[:], T["decay"]), (lalpha[:], T["log_alpha"])):
                e.dma_start(dst, src).then_inc(s_c, 16)
            for dst, src in ((wq, "Wq"), (wkv[:, :, 0:HD], "Wk"), (wkv[:, :, HD:2 * HD], "Wv"), (wo, "Wo"),
                             (ww, "WwT"), (wr, "WrT"), (wg, "Wg")):
                e.dma_start(dst[:] if src not in ("Wk", "Wv") else dst,
                            T[src].rearrange("(c p) n -> p c n", p=P)).then_inc(s_w, 16)
            e.dma_start(bq[:], T["bq"]).then_inc(s_w, 16)
            e.dma_start(bo[:], T["bo"]).then_inc(s_w, 16)
            e.dma_start(bkv[:, 0:HD], T["bk"]).then_inc(s_w, 16)
            e.dma_start(bkv[:, HD:2 * HD], T["bv"]).then_inc(s_w, 16)
            e.wait_ge(s_sp, 1)
            e.dma_start(T["disp"].rearrange("(n p) d -> p n d", p=P),
                        xn3[:].unsqueeze(1).to_broadcast([P, ROWS // P + 1, D])).then_inc(s_zero, 16)
            run(e, "sp")
            for l in all_lanes:
                if l.per:
                    e.wait_ge(l.sem, B * l.per)

        @block.gpsimd
        def _(e):
            e.memset(xn3[:], 0.0).then_inc(s_sp, 1)
            e.memset(mhalf[:], -0.5).then_inc(s_sp, 1)
            e.memset(eps[:], EPS).then_inc(s_sp, 1)
            e.memset(before[:], 0.0).then_inc(s_sp, 1)
            e.memset(rkT[:, :, 0:1], 0.0).then_inc(s_sp, 1)
            for q in (0, 1):
                e.memset(kv[q][:, :, 2 * HD:2 * HD + 1], 1.0).then_inc(s_sp, 1)
            e.wait_ge(s_sp, 7)
            e.wait_ge(s_w, 16 * N_W)
            e.wait_ge(s_c, 64)
            e.wait_ge(s_zero, 16)
            e.wait_ge(s_setup, SETUP)
            run(e, "pool")

        @block.scalar
        def _(e):
            e.wait_ge(s_c, 64)
            e.activation(logg[:], decay[:], ACT.Exp, scale=-1.0).then_inc(s_sa, 1)
            e.activation(alpha[:], lalpha[:], ACT.Exp).then_inc(s_sa, 1)
            e.wait_ge(s_setup, 2)
            e.activation(logg[:], logg[:], ACT.Ln).then_inc(s_sa, 1)
            e.wait_ge(s_sa, 3)
            e.activation(gamma[:], logg[:], ACT.Exp).then_inc(s_sa, 1)
            for n, (dst, which) in enumerate(((decT, C_EXPO), (decI, C_EXPO_I))):
                for h in range(DH):
                    e.activation(dst[:, h, :], cst[:, which, :], ACT.Exp, scale=logg[:, h:h + 1]).then_inc(s_sa, 1)
            e.wait_ge(s_setup, SETUP)
            e.wait_ge(s_w, 16 * N_W)
            run(e, "act")

        @block.vector
        def _(e):
            n = [0]

            def own(ins):
                n[0] += 1
                ins.then_inc(s_setup, 1)
                e.wait_ge(s_setup, n[0])
            e.wait_ge(s_sa, 2)
            own(e.tensor_scalar(logg[:], logg[:], 1.0, None, ALU.add))
            own(e.reciprocal(logg[:], logg[:]))
            e.wait_ge(s_sa, 4 + 2 * DH)
            for h in range(DH):
                own(e.tensor_tensor(decT[:, h, :], decT[:, h, :], cst[:, C_UPPER, :], ALU.mult))
                own(e.scalar_tensor_tensor(decI[:, h, :], decI[:, h, :], alpha[:, h:h + 1], cst[:, C_UPPER, :],
                                           ALU.mult, ALU.mult))
                own(e.tensor_tensor(dec1T[:, h, :], decT[:, h, :], cst[:, C_PAIR_T, :], ALU.mult))
            for h in range(DH):
                own(e.tensor_scalar(dec1[:, h, :], cst[:, C_PAIR, :], gamma[:, h:h + 1], None, ALU.mult))
            e.wait_ge(s_w, 16 * N_W)
            for q in (0, 1):
                own(e.memset(kT[q][3 * HD:3 * HD + 1, :].bitcast(F32), 1.0))
            own(e.tensor_scalar(bq[:], bq[:], SCALE, None, ALU.mult))
            assert n[0] == SETUP
            e.wait_ge(s_sp, 7)
            run(e, "dve")

        @block.tensor
        def _(e):
            e.wait_ge(s_setup, SETUP)
            e.wait_ge(s_w, 16 * N_W)
            e.wait_ge(s_sp, 7)
            run(e, "pe")


def second_pipeline(nc, T):
    with ExitStack() as ctx:
        def sb(name, shape, dt=F32):
            return ctx.enter_context(nc.sbuf_tensor(name, shape, dt))

        def lane(name):
            return Lane(ctx.enter_context(nc.semaphore(name)))

        bank = [ctx.enter_context(nc.psum_tensor(f"ebank{i}", [P, 512], F32)) for i in range(8)]
        T_BANK, H_BANK, Y_BANK = bank[0], bank[1:5], bank[5:7]
        w1 = [sb(f"w1{i}", [P, DC, F]) for i in range(2)]
        w2 = [sb(f"w2{i}", [P, FT, D]) for i in range(2)]
        dis = [sb(f"dis{i}", [P, D]) for i in range(2)]
        dT = [sb(f"dT{i}", [P, DC, P]) for i in range(2)]
        hT = [sb(f"hT{i}", [P, 4 * P]) for i in range(4)]
        eo = [sb(f"eo{i}", [P, D]) for i in range(2)]
        ident = sb("eident", [P, P])
        lanes = {("expert", e): lane(f"expert_{e}") for e in ("pe", "dve", "act", "pool")}
        L_w1 = [[lane(f"w1_in{i}{j}") for j in range(2)] for i in range(2)]
        L_w2 = [[lane(f"w2_in{i}{j}") for j in range(2)] for i in range(2)]
        L_d, L_y = [lane(f"rows_in{i}") for i in range(2)], [lane(f"rows_out{i}") for i in range(2)]
        s_id = ctx.enter_context(nc.semaphore("ident_in"))
        ev, load, comp = {}, {}, {}
        for q in (0, 1):
            names = ev
            ld = Stage("load", lanes, names)
            cp = Stage("expert", lanes, names if q == 0 else {})
            if q:
                for l in lanes.values():
                    l.per, l.n = l.n, 0
            H = F // 2
            ld.at(0.0)
            ld.dma("sp", lambda e, b, q=q: e.dma_start(dis[q][:], T["disp"].rearrange("(n p) d -> n p d", p=P)[
                bass.ds(b, 1)].rearrange("o p d -> p (o d)")), f"rows{q}", L_d[q], after=[("dTp", 2)])
            for j in range(2):
                ld.at(1.0 + j)
                ld.dma("sp", lambda e, b, q=q, j=j: e.dma_start(
                    w1[q][:, :, j * H:(j + 1) * H], T["w1"][bass.ds(b, 1)].rearrange(
                        "o (c p) f -> p (o c) f", p=P)[:, :, j * H:(j + 1) * H]), f"w1{q}{j}", L_w1[q][j],
                    after=[(f"H{2 * j + 1}", 2)])
            for j in range(2):
                ld.at(3.0 + j)
                ld.dma("sp", lambda e, b, q=q, j=j: e.dma_start(
                    w2[q][:, 8 * j:8 * j + 8, :], T["w2"][bass.ds(b, 1)].rearrange(
                        "o (h c p) m -> h p (o c) m", p=P, h=2)[j]), f"w2{q}{j}", L_w2[q][j],
                    after=[(f"Y{2 * j + 1}", 2)])

            def turn(e, b, q=q):
                for c in range(DC):
                    i = e.transpose(T_BANK[:, c * P:(c + 1) * P], dis[q][:, c * P:(c + 1) * P], ident[:])
                return i
            cp.at(0.0)
            cp.step("pe", turn, "dTp", [f"rows{q}", ("dT", 1)])
            cp.step("dve", lambda e, b, q=q: e.tensor_copy(dT[q][:].rearrange("p c t -> p (c t)"), T_BANK[:]), "dT",
                    ["dTp", ("H3", 2)])

            def up(e, b, g, q):
                for f in range(4):
                    for c in range(DC):
                        i = e.matmul(H_BANK[g][:, f * P:(f + 1) * P],
                                     w1[q][:, c, (4 * g + f) * P:(4 * g + f + 1) * P], dT[q][:, c, :],
                                     start=c == 0, stop=c == DC - 1)
                return i

            def down(e, b, g, q):
                for f in range(4):
                    i = e.matmul(Y_BANK[q][:], hT[g][:, f * P:(f + 1) * P], w2[q][:, 4 * g + f, :],
                                 start=g == 0 and f == 0, stop=g == 3 and f == 3)
                return i

            for g in range(4):
                cp.at(1.0 + g)
                cp.step("pe", lambda e, b, g=g, q=q: up(e, b, g, q), f"H{g}",
                        [f"w1{q}{g // 2}", "dT", (f"relu{g}", 1)])
                if g % 2:
                    cp.step("act", lambda e, b, g=g: e.activation(hT[g][:], H_BANK[g][:], ACT.Relu), f"relu{g}",
                            [f"H{g}", (f"Y{g}", 1)])
                else:
                    cp.step("dve", lambda e, b, g=g: e.tensor_scalar(hT[g][:], H_BANK[g][:], 0.0, None, ALU.max),
                            f"relu{g}", [f"H{g}", (f"Y{g}", 1)])
                if g:
                    cp.step("pe", lambda e, b, g=g - 1, q=q: down(e, b, g, q), f"Y{g - 1}",
                            [f"relu{g - 1}", f"w2{q}{(g - 1) // 2}"] + ([("eo", 2)] if g == 1 else []))
            cp.at(5.0)
            cp.step("pe", lambda e, b, q=q: down(e, b, 3, q), "Y3", ["relu3", f"w2{q}1"])
            cp.step("act", lambda e, b, q=q: e.copy(eo[q][:], Y_BANK[q][:]), "eo", ["Y3", (f"out{q}", 2)])
            cp.dma("sp", lambda e, b, q=q: e.dma_start(T["eo"].rearrange("(n p) d -> n p d", p=P)[
                bass.ds(b, 1)].rearrange("o p d -> p (o d)"), eo[q][:]), f"out{q}", L_y[q], after=["eo"])
            for n, v in cp.events.items():
                ev.setdefault(n, v)
            load[q], comp[q] = ld, cp
        for (_, l) in lanes.items():
            assert l.per == l.n
        halves = L_d + L_y + [l for x in L_w1 + L_w2 for l in x]
        for l in halves:
            l.per = 8
        for n, (l, k) in list(ev.items()):
            if l in halves:
                ev[n] = (l, 16 - 8 * int(n[-1 if l in L_d + L_y else -2]))

        def run(e, eng):
            def parts(r, i):
                b = [(load, i + 1), (comp, i)]
                if r is None:
                    return [(s[n % 2], n) for s, n in b if 0 <= n < E]
                return [(s[n % 2], (r, n)) for s, n in b]
            for i in (-1, 0, 1):
                issue(e, eng, parts(None, i), ev)
            with e.Fori(2, E - 3, 2) as r:
                bases = {}
                for d in (0, 1):
                    issue(e, eng, parts(r, d), ev, bases)
            for i in (E - 2, E - 1):
                issue(e, eng, parts(None, i), ev)

        block = ctx.enter_context(nc.Block())

        @block.sync
        def _(e):
            e.dma_start(ident[:], T["consts"][:, C_IDENT, :]).then_inc(s_id, 16)
            run(e, "sp")
            for l in list(lanes.values()) + halves:
                if l.per:
                    e.wait_ge(l.sem, E * l.per)

        @block.tensor
        def _(e):
            e.wait_ge(s_id, 16)
            run(e, "pe")

        @block.scalar
        def _(e):
            run(e, "act")

        @block.vector
        def _(e):
            run(e, "dve")


def last_part(nc, T, keep):
    N = 4
    with ExitStack() as ctx:
        gidx_all, gate_all = keep
        rows = [ctx.enter_context(nc.sbuf_tensor(f"rows{i}", [P, D], F32)) for i in range(N)]
        res = [ctx.enter_context(nc.sbuf_tensor(f"res{i}", [P, D], F32)) for i in range(N)]
        index = ctx.enter_context(nc.sbuf_tensor("index", [P, B], U32))
        s_rows, s_res, s_out = ([ctx.enter_context(nc.semaphore(f"{n}{i}")) for i in range(N)]
                                for n in ("s_rows", "s_res", "s_out"))
        s_sum, s_index = ctx.enter_context(nc.semaphore("s_sum")), ctx.enter_context(nc.semaphore("s_index"))
        block = ctx.enter_context(nc.Block())

        @block.gpsimd
        def _(e):
            e.wait_ge(s_index, 1)
            for b in range(B):
                if b >= N:
                    e.wait_ge(s_sum, b - N + 1)
                e.indirect_dma_start(out=rows[b % N][:], out_offset=None, in_=T["eo"][:],
                                     in_offset=bass.IndirectOffsetOnAxis(ap=index[:, b:b + 1], axis=0)
                                     ).then_inc(s_rows[b % N], 16)

        @block.sync
        def _(e):
            for b in range(B + N - 1):
                if b < B:
                    if b >= N:
                        e.wait_ge(s_out[b % N], 16 * (b // N))
                    e.dma_start(res[b % N][:], T["x2"][b]).then_inc(s_res[b % N], 16)
                if b >= N - 1:
                    o = b - N + 1
                    e.wait_ge(s_sum, o + 1)
                    e.dma_start(T["out"][o], res[o % N][:]).then_inc(s_out[o % N], 16)
            for i in range(N):
                e.wait_ge(s_out[i], 16 * (B // N))

        @block.vector
        def _(e):
            e.tensor_copy(index[:], gidx_all[:]).then_inc(s_index, 1)
            for b in range(B):
                e.wait_ge(s_rows[b % N], 16 * (b // N + 1))
                e.wait_ge(s_res[b % N], 16 * (b // N + 1))
                e.scalar_tensor_tensor(res[b % N][:], rows[b % N][:], gate_all[:, b:b + 1], res[b % N][:],
                                       ALU.mult, ALU.add).then_inc(s_sum, 1)


def program(nc, T):
    with ExitStack() as ctx:
        keep = [ctx.enter_context(nc.sbuf_tensor(n, [P, B], F32)) for n in ("gidx_all", "gate_all")]
        first_pipeline(nc, T, keep)
        nc.all_engine_barrier()
        second_pipeline(nc, T)
        nc.all_engine_barrier()
        last_part(nc, T, keep)


def tables():
    c = np.zeros((P, NCONST, P), np.float32)
    r, q = np.arange(P)[:, None], np.arange(P)[None, :]
    c[:, C_IDENT] = r == q
    same = r // CH == q // CH
    c[:, C_EXPO] = np.where(r < q, np.where(same, q - r, CH - 1 - r), 0)
    c[:, C_EXPO_I] = np.where(r < q, np.where(same, q - r, q - 1 - r), 0)
    c[:, C_UPPER] = r < q
    c[:, C_PAIR] = -1.0 * ((r % 2 == 1) & (q == r - 1))
    c[:, C_PAIR_T] = -1.0 * ((q % 2 == 1) & (r == q - 1))
    c[:, C_ONES] = 1.0
    c[:, C_DUMP] = ROWS + r
    for n in range(6):
        s = 2 << n
        c[:, C_LEVEL + n] = (r // (2 * s) == q // (2 * s)) & (r % (2 * s) >= s) & (q % (2 * s) < s)
    return c


def kernel(**inputs):
    from concourse import bacc
    from concourse.bass_utils import run_bass_kernel_spmd

    nc = bacc.Bacc("TRN2", target_bir_lowering=False, num_devices=1)
    g = {k: np.asarray(v) for k, v in inputs.items()}

    def rows(v):
        return np.ascontiguousarray(np.broadcast_to(v[None, :], (P, v.shape[0])))
    arrays = {
        "x": g["x"], "ctx": g["ctx_1024"], "Wq": g["L0_xattn_Wq"], "Wk": g["L0_xattn_Wk"],
        "Wv": g["L0_xattn_Wv"], "Wo": g["L0_xattn_Wo"], "bq": rows(g["L0_xattn_bq"]),
        "bk": rows(g["L0_xattn_bk"]), "bv": rows(g["L0_xattn_bv"]), "bo": rows(g["L0_xattn_bo"]),
        "WwT": np.ascontiguousarray(g["L0_attn_Ww"].T), "WrT": np.ascontiguousarray(g["L0_attn_Wr"].T),
        "decay": rows(g["L0_attn_decay"]), "log_alpha": rows(g["L0_attn_log_alpha"]), "Wg": g["L0_ffn_Wg"],
        "w1": g["L0_ffn_w1"], "w2": g["L0_ffn_w2"], "consts": tables(),
        "iota": rows(np.arange(E, dtype=np.float32) - E),
    }
    T = {k: nc.dram_tensor(f"in_{k}", v.shape, F32, kind="ExternalInput").ap() for k, v in arrays.items()}
    T["out"] = nc.dram_tensor("out", (B, P, D), F32, kind="ExternalOutput").ap()
    T["x2"] = nc.dram_tensor("x2_scratch", (B, P, D), F32, kind="Internal").ap()
    T["disp"] = nc.dram_tensor("dispatched", (ROWS + P, D), F32, kind="Internal").ap()
    T["eo"] = nc.dram_tensor("expert_rows", (ROWS, D), F32, kind="Internal").ap()
    program(nc, T)
    r = run_bass_kernel_spmd(nc, [{f"in_{k}": v for k, v in arrays.items()}], core_ids=[0])
    return r.results[0]["out"]
```

```python
from contextlib import ExitStack

import numpy as np
import concourse.bass as bass
from concourse import mybir

F32, F32R, U32 = mybir.dt.float32, mybir.dt.float32r, mybir.dt.uint32
ALU, ACT, AX = mybir.AluOpType, mybir.ActivationFunctionType, mybir.AxisListType

P = 128
B, S, D = 16, 2048, 512
NH, HD = 16, 32
DC = D // P
KB = S // P
HG = NH // 4
DH = 4
CH = 64
E, F = 16, 2048
FT = F // P
CAP = (B * P + E - 1) // E
ROWS = E * CAP
EPS = 1e-5
SCALE = float(HD) ** -0.5
C_IDENT, C_UPPER, C_PAIR, C_PAIR_T, C_ONES, C_DUMP, C_LEVEL = range(7)
NCONST = C_LEVEL + 6
C_EXPO, C_EXPO_I = NCONST, NCONST + 1
NF, NHI, NL = 2, 4, 4
T0, TSTEP = 13.0, 2.3
LAG = 2.4
UNITS = HG * KB


class Lane:

    def __init__(self, sem):
        self.sem, self.per, self.n = sem, None, 0


class Stage:

    def __init__(self, name, lanes, events, clock=0.0):
        self.name, self.lanes, self.events, self.t, self.steps = name, lanes, events, clock, []

    def at(self, t):
        assert t >= self.t - 1e-9, (self.name, self.t, t)
        self.t = t

    def step(self, eng, fn, name=None, after=(), lane=None, by=1):
        if lane is None:
            lane = self.lanes[(self.name, eng)]
        if name is not None:
            lane.n += by
            assert name not in self.events, name
            self.events[name] = (lane, lane.n)
        self.steps.append((self.t, eng, fn, name is not None and (lane, by), tuple(after)))

    def stretch(self, end):
        self.steps = [(s[0] * end / self.t,) + s[1:] for s in self.steps]

    def dma(self, eng, fn, name, lane, after=()):
        self.step(eng, fn, name, after, lane, 16)


def issue(e, eng, parts, events, bases=None):
    merged = sorted(((s[0], n, j, s, b) for n, (st, b) in enumerate(parts)
                     for j, s in enumerate(st.steps)), key=lambda m: m[:3])
    for _, _, _, (_, on, fn, mark, after), b in merged:
        if on != eng:
            continue
        need = {}
        for a in after:
            name, ago = a if isinstance(a, tuple) else (a, 0)
            lane, k = events[name]
            if not isinstance(b, int) or b >= ago:
                off = b if isinstance(b, int) else b[1]
                need[lane] = max(need.get(lane, -10**6), (off - ago) * lane.per + k)
        for lane, n in need.items():
            if not isinstance(b, int):
                if lane not in bases:
                    bases[lane] = e.snap(b[0] * lane.per)
                n = bases[lane] + n
            e.wait_ge(lane.sem, n)
        ins = fn(e, b if isinstance(b, int) else b[0] + b[1])
        if mark:
            ins.then_inc(mark[0].sem, mark[1])


def first_pipeline(nc, T, keep):
    with ExitStack() as ctx:
        def sb(name, shape, dt=F32):
            return ctx.enter_context(nc.sbuf_tensor(name, shape, dt))

        def lane(name):
            return Lane(ctx.enter_context(nc.semaphore(name)))

        bank = [ctx.enter_context(nc.psum_tensor(f"bank{i}", [P, 512], F32)) for i in range(8)]
        A_BANK, B_BANK, PV_BANK, T_BANK, KV_BANK, POST = bank[0:2], bank[2:4], bank[4], bank[5], bank[6], bank[7]

        cst = sb("cst", [P, NCONST, P])
        ident = cst[:, C_IDENT, :]
        iota = sb("iota", [P, E])
        wq, wo, ww, wr = (sb(n, [P, DC, D]) for n in ("wq", "wo", "ww", "wr"))
        wkv2 = sb("wkv2", [P, DC, 4 * HD], F32R)
        wg = sb("wg", [P, DC, E])
        bq, bo, bkv = sb("bq", [P, D]), sb("bo", [P, D]), sb("bkv", [2 * HD, 1])
        decay, lalpha = sb("decay", [P, DH]), sb("lalpha", [P, DH])
        logg, alpha, gamma = sb("logg", [P, DH]), sb("alpha", [P, DH]), sb("gamma", [P, DH])
        decT, decI, dec1 = (sb(n, [P, DH, P]) for n in ("decT", "decI", "dec1"))
        mhalf, eps = sb("mhalf", [P, DH]), sb("eps", [P, 1])
        pad_dve, pad_pool = sb("pad_dve", [P, 1]), sb("pad_pool", [P, 1])
        cx = [sb(f"cx{c}", [P, 4, D]) for c in range(4)]
        cxh, cxl = sb("cxh", [P, DC, 512], F32R), sb("cxl", [P, DC, 512], F32R)
        kvlow, kvs = sb("kvlow", [2 * HD, 512]), sb("kvs", [P, 512])
        v3 = [sb(f"v3{i}", [P, KB, 2 * HD + 1], F32R) for i in range(2)]
        kT = [sb(f"kT{i}", [P, S], F32R) for i in range(2)]
        qT = [sb(f"qT{i}", [P, NH * P], F32R) for i in range(2)]
        xin, xnT, qf = sb("xin", [P, D]), sb("xnT", [P, DC, P]), sb("qf", [P, D])
        xn = xin
        q3 = sb("q3", [P, NH, 3 * HD])
        st1, mv1, rs1 = sb("st1", [P, 6]), sb("mv1", [P, 2]), sb("rs1", [P, 2])
        pf = [sb(f"pf{i}", [P, 512]) for i in range(NF)]
        ph = [sb(f"ph{i}", [P, 512], F32R) for i in range(NHI)]
        pl = [sb(f"pl{i}", [P, 512], F32R) for i in range(NL)]
        oS, oN, oSum = sb("oS", [2 * HD + 1, 512]), sb("oN", [P, 4, 2 * HD + 1]), sb("oSum", [P, 4, HD])
        mpart = [sb(f"mpart{i}", [P, 16]) for i in range(2)]
        mneg = sb("mneg", [P, 4])
        mrow = [sb(f"mrow{i}", [4, P], F32R) for i in range(2)]
        rsum = sb("rsum", [P, 4])
        att = [sb(f"att{i}", [P, D]) for i in range(2)]
        xr, x1, xn2, x12, rk, V, Y, x2, xn3, turned = (
            sb(n, [P, D]) for n in ("xr", "x1", "xn2", "x12", "rk", "V", "Y", "x2", "xn3", "turned"))
        XT, MT, X, IT, Vn = xr, x1, xn2, rk, Y
        oT1 = xn2T = oT2 = xn3T = turned
        wkv = V[:, 0:2 * HD * DC].rearrange("p (c n) -> p c n", c=DC)
        expo = Y[:, 0:2 * P].rearrange("p (k t) -> p k t", k=2)
        rkT = sb("rkT", [P, DH, P + 1])
        st2, mv2, rs2 = sb("st2", [P, 6]), sb("mv2", [P, 2]), sb("rs2", [P, 2])
        st3, mv3, rs3 = sb("st3", [P, 6]), sb("mv3", [P, 2]), sb("rs3", [P, 2])
        ss, rn = sb("ss", [P, DH]), sb("rn", [P, DH])
        lg, eg, oh, oh2 = (sb(n, [P, E]) for n in ("lg", "eg", "oh", "oh2"))
        before = sb("before", [P, E])
        sc = sb("sc", [P, 12])
        sidx = sb("sidx", [P, 1], U32)
        gidx_all, gate_all = keep

        lanes = {(s, e): lane(f"{s}_{e}") for s in ("prep", "attn", "tail", "max", "post") for e in ("pe", "dve", "act", "pool")}
        L_ctx = [lane(f"ctx_in{c}") for c in range(4)]
        L_x, L_xr, L_x2, L_scat = lane("x_in"), lane("xr_in"), lane("x2_out"), lane("scatter_out")
        L_mrow = [lane(f"mrow_dma{g}") for g in range(HG)]
        ev = {}

        def aggregate(e, out, in_):
            e.memset(pad_dve[:], 0.0)
            return e.bn_aggr(out, in_)

        def scatter(e):
            e.tensor_tensor(pad_pool[:], mhalf[:, 0:1], mhalf[:, 0:1], ALU.mult)
            return e.indirect_dma_start(
                out=T["disp"][:], out_offset=bass.IndirectOffsetOnAxis(ap=sidx[:, 0:1], axis=0), in_=xn3[:],
                in_offset=None)

        def transposes(e, out, src, n=4, m=P):
            for j in range(n):
                i = e.transpose(out[0:m, j * P:(j + 1) * P], src(j), ident)
            return i

        def copy(on, e, out, in_):
            return e.copy(out, in_) if on == "act" else e.tensor_copy(out, in_)

        load = Stage("load", lanes, ev)
        for c in range(4):
            load.at(T0 + TSTEP * (4 * c + 3) + 0.5)
            load.dma("sp", lambda e, b, c=c: e.dma_start(cx[c][:], T["ctx"][bass.ds(b, 1)].rearrange(
                "o (p c k) d -> c p (o k) d", c=4, k=4)[c]), f"ctx{c}", L_ctx[c],
                after=[(f"T{4 * c + 3}", 1)])

        def prep_steps(st, q):
            st.at(0.0)
            st.dma("sp", lambda e, b: e.dma_start(xin[:], T["x"][bass.ds(b, 1)].rearrange("o p d -> p (o d)")),
                   "x", L_x, after=[("xnTp", 1)])
            st.at(2.0)
            st.step("dve", lambda e, b: e.bn_stats(st1[:], xin[:]), "st1", ["x"])
            st.step("dve", lambda e, b: aggregate(e, mv1[:], st1[:]), "mv1", ["st1"])
            st.step("pool", lambda e, b: e.tensor_tensor(rs1[:, 0:1], mv1[:, 1:2], eps[:, 0:1], ALU.add), "ve1", ["mv1"])
            st.step("pool", lambda e, b: e.tensor_tensor(rs1[:, 1:2], rs1[:, 0:1], mhalf[:, 0:1], ALU.pow), "rs1",
                    ["ve1"])
            st.at(3.5)
            st.step("dve", lambda e, b: e.tensor_scalar(xn[:], xin[:], mv1[:, 0:1], rs1[:, 1:2], ALU.subtract,
                                                        ALU.mult), "xn", ["mv1", "rs1", ("xnTp", 1)])
            st.at(4.5)
            st.step("pe", lambda e, b: transposes(e, T_BANK, lambda j: xn[:, j * P:(j + 1) * P]), "xnTp",
                    ["xn", ("vl3", 1)])
            st.at(5.0)
            st.step("act", lambda e, b: e.copy(xnT[:].rearrange("p c t -> p (c t)"), T_BANK[:]), "xnT",
                    ["xnTp"])

            for c in range(DC):
                st.at(5.5 + 0.6 * c)
                st.step("pe", lambda e, b, c=c: e.matmul(KV_BANK[:], xnT[:, c, :], wq[:, c, :], start=c == 0,
                                                         stop=c == DC - 1), "Qp" if c == DC - 1 else None,
                        ["xnT", ("kvs3", 1)] if c == 0 else [])
            st.at(7.6)
            st.step("dve", lambda e, b: e.scalar_tensor_tensor(qf[:], KV_BANK[:], SCALE, bq[:], ALU.mult, ALU.add),
                    "qf", ["Qp", ("qh", 1)])
            q4, qf4 = q3[:], qf[:].rearrange("p (h d) -> p h d", h=NH)
            qh = q4.bitcast(F32R)
            st.step("dve", lambda e, b: e.tensor_copy(qh[:, :, 0:HD], qf4), "qh0", ["qf", ("qTp3", 1)])
            st.step("act", lambda e, b: e.copy(qh[:, :, HD:2 * HD], qf4), "qh", ["qf", ("qTp3", 1)])
            st.step("dve", lambda e, b: e.tensor_tensor(q4[:, :, 2 * HD:3 * HD], qf4, q4[:, :, 0:HD], ALU.subtract),
                    "ql", ["qh0"])
            for g in range(HG):
                st.at(9.0 + g)
                st.step("pe", lambda e, b, g=g: transposes(e, T_BANK, lambda j: q3[:, 4 * g + j, :], 4, 3 * HD),
                        f"qTp{g}", ["qh", "ql", "xnT" if g == 0 else f"qT{g - 1}"])
                st.at(9.3 + g)
                on = "act" if g % 2 else "dve"
                st.step(on, lambda e, b, g=g, on=on: copy(on, e, qT[q][0:3 * HD, g * 512:(g + 1) * 512], T_BANK[0:3 * HD, :]),
                        f"qT{g}", [f"qTp{g}", (f"B{UNITS - 1}", 2)])
            for k in range(KB):
                t = T0 + TSTEP * k
                c, kk = divmod(k, 4)
                cols = slice(kk * P, (kk + 1) * P)
                bank3 = T_BANK[:].rearrange("p (c t) -> p c t", c=DC)
                st.at(t)
                prev = "qT3" if k == 0 else (f"vl{c - 1}" if kk == 0 else f"cxl{k - 1}")
                st.step("pe", lambda e, b, c=c, kk=kk: transposes(
                    e, T_BANK, lambda j: cx[c][:, kk, j * P:(j + 1) * P]), f"T{k}", [f"ctx{c}", prev])
                st.at(t + 0.2)
                st.step("act", lambda e, b, cols=cols, bank3=bank3: e.copy(cxh[:, :, cols], bank3), f"cxh{k}",
                        [f"T{k}"] + ([f"KVp{c - 1}" if c else ("KVp3", 1)] if kk == 0 else []))
                st.step("dve", lambda e, b, cols=cols, bank3=bank3: e.tensor_tensor(
                    cxl[:, :, cols], bank3, cxh[:, :, cols].bitcast(F32), ALU.subtract), f"cxl{k}", [f"cxh{k}"])
                if kk < 3:
                    continue

                def kv_proj(e, b):
                    for j in range(DC):
                        e.matmul(KV_BANK[:], wkv2[:, j, :], cxh[:, j, :], start=j == 0, stop=False)
                        i = e.matmul(KV_BANK[:], wkv2[:, j, :], cxl[:, j, :], start=False, stop=j == DC - 1)
                    return i
                st.at(t + 1.0)
                st.step("pe", kv_proj, f"KVp{c}", [f"cxl{k}", f"kvs{c - 1}" if c else "qf"])
                st.at(t + 1.3)
                st.step("act", lambda e, b: e.copy(kvlow[:], KV_BANK[2 * HD:4 * HD, :]), f"kvlow{c}",
                        [f"KVp{c}", f"kvs{c - 1}" if c else ("kvs3", 1)])
                st.step("dve", lambda e, b: e.scalar_tensor_tensor(
                    kvs[0:2 * HD, :], KV_BANK[0:2 * HD, :], bkv[:, 0:1], kvlow[:], ALU.add, ALU.add), f"kvs{c}",
                    [f"kvlow{c}", f"vTp{c - 1}" if c else ("vTp3", 1), f"kl{c - 1}" if c else ("kl3", 1),
                     f"kh{c - 1}" if c else ("kh3", 1)])
                ks = slice(c * 512, (c + 1) * 512)
                st.step("act", lambda e, b, ks=ks: e.copy(kT[q][0:HD, ks], kvs[0:HD, :]), f"kh{c}",
                        [f"kvs{c}", (f"B{UNITS - 1}", 2)])
                st.step("dve", lambda e, b, ks=ks: e.tensor_copy(kT[q][2 * HD:3 * HD, ks], kvs[0:HD, :]),
                        f"kh2{c}", [f"kvs{c}", (f"B{UNITS - 1}", 2)])
                st.step("dve", lambda e, b, ks=ks: e.tensor_tensor(
                    kT[q][HD:2 * HD, ks], kvs[0:HD, :], kT[q][0:HD, ks].bitcast(F32), ALU.subtract),
                    f"kl{c}", [f"kh{c}"])
                vb = T_BANK[:].rearrange("p (k n) -> p k n", k=4)[:, :, HD:2 * HD]
                vk = slice(4 * c, 4 * c + 4)

                st.at(t + 1.9)
                st.step("pe", lambda e, b: transposes(e, T_BANK, lambda j: kvs[:, j * P:(j + 1) * P]), f"vTp{c}",
                        [f"kvs{c}", f"cxl{k}"])
                st.step("act", lambda e, b, vb=vb, vk=vk: e.copy(v3[q][:, vk, 0:HD], vb), f"vh{c}",
                        [f"vTp{c}", (f"PV{UNITS - 1}", 2)])
                st.step("dve", lambda e, b, vb=vb, vk=vk: e.tensor_tensor(
                    v3[q][:, vk, HD:2 * HD], vb, v3[q][:, vk, 0:HD].bitcast(F32), ALU.subtract), f"vl{c}",
                    [f"vh{c}"])
            maxima(st, 0, q, 51.3, 0.6)

        def maxima(st, g, q, t0, pace=0.7):
            for n in range(17):
                use = 17 * g + n
                a = A_BANK[use % 2]
                prev = 17 * g + n - 2
                w = [f"A_free{prev}"] if prev >= 0 else [(f"A_free{prev + 17 * HG}", 1)]
                if n < 16:
                    h, c = divmod(n, 4)
                    st.at(t0 + pace * n)
                    st.step("pe", lambda e, b, h=h, c=c, a=a: e.matmul(
                        a[:], qT[q][0:3 * HD, (4 * g + h) * P:(4 * g + h + 1) * P],
                        kT[q][0:3 * HD, c * 512:(c + 1) * 512], start=True, stop=True), f"A{use}",
                        w + ([f"qT{g}", "kh3", "kh23", "kl3", "qT3"] if n == 0 else []))
                    st.at(t0 + pace * n + 0.3)
                    st.step("dve", lambda e, b, n=n, a=a: e.tensor_reduce(mpart[g % 2][:, n:n + 1], a[:], AX.X,
                                                                          ALU.max), f"A_free{use}", [f"A{use}"])
                else:
                    st.step("dve", lambda e, b: e.tensor_reduce(
                        mneg[:], mpart[g % 2][:].rearrange("p (h c) -> p h c", h=4), AX.X, ALU.max, negate=True),
                        f"mneg{g}", [f"A_free{use - 1}", (f"A{17 * g - 1}", 0) if g else (f"A{17 * HG - 1}", 1)])
                    st.at(t0 + pace * n + 0.8)
                    st.step("pe", lambda e, b, a=a: e.transpose(a[0:4, 0:P], mneg[:], ident), f"A{use}",
                            w + [f"mneg{g}"])
                    st.at(t0 + pace * n + 1.0)
                    st.step("act", lambda e, b, a=a: e.copy(mrow[g % 2][:], a[0:4, 0:P]), f"A_free{use}",
                            [f"A{use}", (f"mrow{g - 2}", 0) if g > 1 else (f"mrow{g + 2}", 1)])
                    st.dma("sp", lambda e, b: e.dma_start(
                        qT[q][3 * HD:3 * HD + 1, g * 512:(g + 1) * 512].bitcast(F32).rearrange(
                            "o (h t) -> o h t", h=4), mrow[g % 2][:].bitcast(F32)), f"mrow{g}", L_mrow[g], after=[f"A_free{use}"])

        def attn_steps(st, tail, q):
            mine = []
            for g in range(HG):
                for k in range(KB):
                    u = g * KB + k

                    def scores(st, g=g, k=k, u=u):
                        w = [f"exp{u - 2}"] if u > 1 else [(f"exp{u - 2 + UNITS}", 1)]
                        if k == 0:
                            w += [f"mrow{g}"]
                        st.step("pe", lambda e, b: e.matmul(
                            B_BANK[u % 2][:], kT[q][0:3 * HD + 1, k * P:(k + 1) * P],
                            qT[q][0:3 * HD + 1, g * 512:(g + 1) * 512], start=True, stop=True), f"B{u}", w)
                    mine.append((u, scores))

                    def expo(st, g=g, k=k, u=u):
                        def free(by, n):
                            return f"{by}{u - n}" if u >= n else (f"{by}{u - n + UNITS}", 1)
                        st.step("act", lambda e, b: e.activation(ph[u % NHI][:], B_BANK[u % 2][:], ACT.Exp),
                                f"exph{u}", [f"B{u}", free("PV", NHI)])
                        st.step("act", lambda e, b: e.activation(pf[u % NF][:], B_BANK[u % 2][:], ACT.Exp),
                                f"exp{u}", [f"B{u}", free("pl", NF)])
                        st.step("pool", lambda e, b: e.tensor_tensor(
                            pl[u % NL][:], pf[u % NF][:], ph[u % NHI][:].bitcast(F32), ALU.subtract),
                            f"pl{u}", [f"exp{u}", free("PV", NL)])
                    mine.append((u + 0.1, expo))

                    def weigh(st, g=g, k=k, u=u):
                        def f(e, b):
                            e.matmul(PV_BANK[0:2 * HD + 1, :], v3[q][:, k, :], ph[u % NHI][:], start=k == 0,
                                     stop=False)
                            return e.matmul(PV_BANK[0:2 * HD + 1, :], v3[q][:, k, :], pl[u % NL][:],
                                            start=False, stop=k == KB - 1)
                        w = [f"pl{u}"]
                        if k == 0:
                            w += [f"oN{g - 1}" if g else (f"oN{HG - 1}", 1), "vl3"]
                        st.step("pe", f, f"PV{u}", w)
                    mine.append((u + LAG + (0.7 if k == 0 else 0.2 if k == 1 else 0), weigh))

                def turn(st, g=g):
                    st.step("act", lambda e, b: e.copy(oS[:], PV_BANK[0:2 * HD + 1, :]), f"oS{g}",
                            [f"PV{g * KB + KB - 1}", f"oTp{g - 1}" if g else (f"oTp{HG - 1}", 1)])

                def turn2(st, g=g):
                    def f(e, b):
                        for j in range(4):
                            i = e.transpose(PV_BANK[:, 65 * j:65 * j + 65], oS[:, j * P:(j + 1) * P],
                                            ident[0:2 * HD + 1, 0:2 * HD + 1])
                        return i
                    st.step("pe", f, f"oTp{g}", [f"oS{g}"])

                def normalise(st, g=g):
                    st.step("dve", lambda e, b: e.tensor_copy(oN[:].rearrange("p h n -> p (h n)"),
                                                              PV_BANK[:, 0:4 * 65]), f"oN{g}", [f"oTp{g}"])
                    st.step("dve", lambda e, b: e.reciprocal(rsum[:], oN[:, :, 2 * HD]), f"rsum{g}", [f"oN{g}"])
                    st.step("dve", lambda e, b: e.tensor_tensor(oSum[:], oN[:, :, 0:HD], oN[:, :, HD:2 * HD],
                                                                ALU.add), f"oSum{g}", [f"oN{g}"])
                    st.step("dve", lambda e, b: e.tensor_tensor(
                        att[q][:, g * P:(g + 1) * P].rearrange("p (h n) -> p h n", h=4), oSum[:],
                        rsum[:].unsqueeze(2).to_broadcast([P, 4, HD]), ALU.mult), f"att{g}",
                        [f"rsum{g}", f"oSum{g}"] + ([("oT1p", 2)] if g == 0 else []))
                end = g * KB + KB - 1 + LAG
                mine += [(end + 0.1, turn), (end + 0.9, turn2), (end + 1.0, normalise)]
            for t, f in sorted(mine, key=lambda m: m[0]):
                to = st if t < UNITS else tail
                to.at(t if t < UNITS else t - UNITS)
                f(to)

        def heads(ap, n=DH):
            return ap.rearrange("p (h t) -> p h t", h=n)

        def post_steps(st, q):
            hop = [3.0]

            def pe(fn, name, after=()):
                st.at(hop[0])
                st.step("pe", fn, name, list(after))
                hop[0] += 0.45

            def then(eng, fn, name, after=()):
                st.at(max(st.t, hop[0]))
                st.step(eng, fn, name, list(after))

            def gap(n=0.85):
                hop[0] = max(hop[0], st.t) + n

            def norm(src, dst, stt, mv, rs, tag, dep, war):
                then("dve", lambda e, b: e.bn_stats(stt[:], src[:]), "st" + tag, [dep])
                then("dve", lambda e, b: aggregate(e, mv[:], stt[:]), "mv" + tag, ["st" + tag])
                then("pool", lambda e, b: e.tensor_tensor(rs[:, 0:1], mv[:, 1:2], eps[:, 0:1], ALU.add), "ve" + tag,
                     ["mv" + tag])
                then("pool", lambda e, b: e.tensor_tensor(rs[:, 1:2], rs[:, 0:1], mhalf[:, 0:1], ALU.pow),
                     "rs" + tag, ["ve" + tag])
                gap(0.6)
                then("dve", lambda e, b: e.tensor_scalar(dst[:], src[:], mv[:, 0:1], rs[:, 1:2], ALU.subtract,
                                                         ALU.mult), "xn" + tag, ["mv" + tag, "rs" + tag] + war)
                gap(0.6)

            def project(name, lhs, w, after):
                for c in range(DC):
                    pe(lambda e, b, c=c: e.matmul(POST[:], lhs[:, c * P:(c + 1) * P], w[:, c, :], start=c == 0,
                                                  stop=c == DC - 1), name if c == DC - 1 else None,
                       after if c == 0 else [])

            def per_head(name, lhs, rhs, after):
                def f(e, b):
                    for h in range(DH):
                        i = e.matmul(POST[:, h * P:(h + 1) * P], lhs(h), rhs(h), start=True, stop=True)
                    return i
                pe(f, name, after)

            def cut(t):
                return lambda h: t[:, h * P:(h + 1) * P]

            st.at(0.0)
            st.dma("sp", lambda e, b: e.dma_start(xr[:], T["x"][bass.ds(b, 1)].rearrange("o p d -> p (o d)")),
                   "xr", L_xr, after=[("Vnp", 1)])
            st.at(2.0)
            st.step("pool", lambda e, b: e.tensor_tensor(xr[:], xr[:], bo[:], ALU.add), "xb", ["xr"])
            pe(lambda e, b: transposes(e, POST, cut(att[q])), "oT1p", ["att3", ("lg", 1)])
            then("act", lambda e, b: e.copy(oT1[:], POST[:]), "oT1", ["oT1p"])
            gap()
            project("x1p", oT1, wo, ["oT1"])
            then("dve", lambda e, b: e.tensor_tensor(x1[:], POST[:], xr[:], ALU.add), "x1", ["x1p", "xb"])
            norm(x1, xn2, st2, mv2, rs2, "2", "x1", [])
            then("pool", lambda e, b: e.tensor_tensor(x12[:], x1[:], xn2[:], ALU.add), "x12", ["xn2"])
            pe(lambda e, b: transposes(e, POST, cut(xn2)), "xn2Tp", ["xn2"])
            then("act", lambda e, b: e.copy(xn2T[:], POST[:]), "xn2T", ["xn2Tp"])
            then("dve", lambda e, b: e.tensor_tensor(rk[:], xn2[:], xn2[:], ALU.mult), "sq", ["xn2"])
            then("dve", lambda e, b: e.tensor_reduce(ss[:], heads(rk[:]), AX.X, ALU.add), "ss", ["sq"])
            then("dve", lambda e, b: e.tensor_scalar(rn[:], ss[:], 1e-24, None, ALU.max), "ssm", ["ss"])
            then("pool", lambda e, b: e.tensor_tensor(rn[:], rn[:], mhalf[:], ALU.pow), "rn", ["ssm"])
            gap(0.5)
            then("dve", lambda e, b: e.tensor_tensor(heads(rk[:]), heads(xn2[:]),
                                                     rn[:].unsqueeze(2).to_broadcast([P, DH, P]), ALU.mult),
                 "rk", ["rn", "ss"])
            gap(0.3)
            project("Vp", xn2T, ww, ["xn2T"])
            then("act", lambda e, b: e.copy(V[:], POST[:]), "V", ["Vp"])
            gap()
            pe(lambda e, b: transposes(e, POST, cut(rk)), "rkTp", ["rk", "V"])
            then("act", lambda e, b: e.copy(rkT[:, :, 1:P + 1], heads(POST[:])), "rkT", ["rkTp"])
            gap()
            per_head("Gp", lambda h: rkT[:, h, 0:P], lambda h: rkT[:, h, 0:P], ["rkT"])
            then("dve", lambda e, b: e.tensor_tensor(MT[:], POST[:], decT[:].rearrange("p h t -> p (h t)"),
                                                     ALU.mult), "MT", ["Gp", "x12"])
            then("dve", lambda e, b: e.tensor_tensor(X[:], POST[:], dec1[:].rearrange("p h t -> p (h t)"),
                                                     ALU.mult), "X1a", ["Gp"])
            then("dve", lambda e, b: e.tensor_tensor(
                heads(XT[:]), heads(MT[:]), cst[:, C_PAIR_T, :].unsqueeze(1).to_broadcast([P, DH, P]), ALU.mult),
                "XT1a", ["MT"])
            idb = ident.unsqueeze(1).to_broadcast([P, DH, P])
            then("pool", lambda e, b: e.tensor_tensor(heads(X[:]), heads(X[:]), idb, ALU.add), "X1", ["X1a"])
            then("pool", lambda e, b: e.tensor_tensor(heads(XT[:]), heads(XT[:]), idb, ALU.add), "XT1", ["XT1a"])
            gap(1.4)
            per_head("Ip", lambda h: rkT[:, h, 0:P], lambda h: rkT[:, h, 1:P + 1], ["XT1a"])
            then("dve", lambda e, b: e.tensor_tensor(IT[:], POST[:], decI[:].rearrange("p h t -> p (h t)"),
                                                     ALU.mult), "IT", ["Ip"])
            gap()
            xs, xts, last = "X1", "XT1", "IT"
            for lv in range(6):
                s = 2 << lv
                per_head(f"Yp{s}", cut(MT), cut(X), ["MT", xs, last])
                then("dve", lambda e, b, lv=lv: e.tensor_tensor(
                    heads(Y[:]), heads(POST[:]), cst[:, C_LEVEL + lv, :].unsqueeze(1).to_broadcast([P, DH, P]),
                    ALU.mult), f"Y{s}", [f"Yp{s}"])
                gap()
                if s < CH:
                    per_head(f"Zp{s}", cut(XT), cut(Y), [f"Y{s}", xts])
                    then("dve", lambda e, b: e.tensor_tensor(X[:], X[:], POST[:], ALU.subtract), f"X{s}",
                         [f"Zp{s}"])
                    gap()
                per_head(f"ZTp{s}", cut(Y), cut(XT), [f"Y{s}", xts] + ([f"X{s}"] if s < CH else []))
                then("dve", lambda e, b: e.tensor_tensor(XT[:], XT[:], POST[:], ALU.subtract), f"XT{s}",
                     [f"ZTp{s}"])
                gap()
                xs, xts, last = f"X{s}", f"XT{s}", f"XT{s}"
            per_head("Vnp", cut(XT), cut(V), ["XT64"])
            then("act", lambda e, b: e.copy(Vn[:], POST[:]), "Vn", ["Vnp"])
            gap()
            per_head("oT2p", cut(Vn), cut(IT), ["Vn"])
            then("act", lambda e, b: e.copy(oT2[:], POST[:]), "oT2", ["oT2p"])
            gap()
            project("x2p", oT2, wr, ["oT2"])
            then("dve", lambda e, b: e.tensor_tensor(x2[:], POST[:], x12[:], ALU.add), "x2",
                 ["x2p", "x12", ("x2out", 1)])
            st.dma("sp", lambda e, b: e.dma_start(T["x2"][bass.ds(b, 1)].rearrange("o p d -> p (o d)"), x2[:]),
                   "x2out", L_x2, after=["x2"])
            norm(x2, xn3, st3, mv3, rs3, "3", "x2", [("scat", 1)])
            pe(lambda e, b: transposes(e, POST, cut(xn3)), "xn3Tp", ["xn3"])
            then("act", lambda e, b: e.copy(xn3T[:], POST[:]), "xn3T", ["xn3Tp"])
            gap()

            def logits(e, b):
                for c in range(DC):
                    i = e.matmul(POST[:, 0:E], xn3T[:, c * P:(c + 1) * P], wg[:, c, :], start=c == 0,
                                 stop=c == DC - 1)
                return i
            pe(logits, "lgp", ["xn3T"])
            then("dve", lambda e, b: e.tensor_copy(lg[:], POST[:, 0:E]), "lg0", ["lgp"])
            then("dve", lambda e, b: e.tensor_reduce(sc[:, 0:1], lg[:], AX.X, ALU.max, negate=True), "lmax",
                 ["lg0", ("eg", 1)])
            then("act", lambda e, b: e.activation(eg[:], lg[:], ACT.Exp, bias=sc[:, 0:1],
                                                  accum_out=sc[:, 1:2]), "eg", ["lmax", ("gate", 1)])
            then("dve", lambda e, b: e.tensor_reduce(sc[:, 2:3], eg[:], AX.X, ALU.max), "emax", ["eg"])
            then("dve", lambda e, b: e.scalar_tensor_tensor(oh2[:], eg[:], sc[:, 2:3], iota[:], ALU.is_ge, ALU.mult),
                 "cand", ["emax"])
            then("dve", lambda e, b: e.tensor_reduce(sc[:, 3:4], oh2[:], AX.X, ALU.min), "best", ["cand"])
            then("dve", lambda e, b: e.tensor_scalar(oh[:], iota[:], sc[:, 3:4], None, ALU.is_equal), "oh",
                 ["best"])
            gap(0.6)

            def places(e, b):
                e.matmul(POST[:, 0:E], cst[:, C_UPPER, :], oh[:], start=True, stop=False)
                return e.matmul(POST[:, 0:E], cst[:, C_ONES, :], before[:], start=False, stop=True)
            pe(places, "locp", ["oh", "lg0", ("before", 1)])
            then("dve", lambda e, b: e.tensor_tensor(oh2[:], POST[:, 0:E], oh[:], ALU.mult), "lg", ["locp"])
            then("dve", lambda e, b: e.tensor_tensor(before[:], before[:], oh[:], ALU.add), "before", ["locp"])
            then("dve", lambda e, b: e.tensor_reduce(sc[:, 4:5], oh2[:], AX.X, ALU.add), "loc", ["lg"])
            then("dve", lambda e, b: e.tensor_scalar(sc[:, 5:6], sc[:, 4:5], float(CAP), None, ALU.is_lt), "valid",
                 ["loc"])
            then("dve", lambda e, b: e.tensor_scalar(sc[:, 6:7], sc[:, 4:5], float(CAP - 1), None, ALU.min), "locc",
                 ["loc"])
            then("dve", lambda e, b: e.tensor_scalar(sc[:, 7:8], sc[:, 3:4], float(CAP), float(E * CAP), ALU.mult,
                                                     ALU.add), "row0", ["best"])
            then("dve", lambda e, b: e.tensor_tensor(sc[:, 8:9], sc[:, 7:8], sc[:, 6:7], ALU.add), "row",
                 ["row0", "locc"])
            then("dve", lambda e, b: e.tensor_tensor(sc[:, 9:10], sc[:, 8:9], cst[:, C_DUMP, 0:1], ALU.subtract),
                 "d0", ["row"])
            then("dve", lambda e, b: e.scalar_tensor_tensor(sc[:, 10:11], sc[:, 9:10], sc[:, 5:6],
                                                            cst[:, C_DUMP, 0:1], ALU.mult, ALU.add), "d1",
                 ["d0", "valid"])
            then("dve", lambda e, b: e.tensor_copy(sidx[:], sc[:, 10:11]), "sidx", ["d1", ("scat", 1)])
            then("dve", lambda e, b: e.tensor_copy(gidx_all[:, bass.ds(b, 1)], sc[:, 8:9]), "gidx", ["row"])
            then("dve", lambda e, b: e.reciprocal(sc[:, 11:12], sc[:, 1:2]), "ginv", ["eg"])
            then("dve", lambda e, b: e.tensor_tensor(gate_all[:, bass.ds(b, 1)], sc[:, 11:12], sc[:, 5:6],
                                                     ALU.mult), "gate", ["ginv", "valid"])
            st.dma("pool", lambda e, b: scatter(e), "scat", L_scat, after=["sidx", "xn3"])

        pre, att_st, tail, post = {}, {}, {}, {}
        all_lanes = list(lanes.values()) + L_ctx + [L_x, L_xr, L_x2, L_scat] + L_mrow
        for q in (0, 1):
            names = ev if q == 0 else {}
            keep_n = [l.n for l in all_lanes]
            if q:
                for l in [l for l in all_lanes if l not in L_ctx]:
                    l.n = 0
            pre[q], post[q] = Stage("prep", lanes, names), Stage("post", lanes, names)
            prep_steps(pre[q], q)
            am, mx, tail[q] = (Stage(n, lanes, names) for n in ("attn", "max", "tail"))
            attn_steps(am, tail[q], q)
            att_st[q] = [am, mx]
            for g in range(1, HG):
                maxima(mx, g, q, 16.0 * (g - 1) + 0.5)
            post_steps(post[q], q)
            post[q].stretch(UNITS - 1.0)
            if q:
                assert keep_n == [l.n for l in all_lanes]
        for l in all_lanes:
            l.per = l.n

        def parts(i, known):
            out = []
            for off, sts in ((2, lambda q: [load]), (1, lambda q: [pre[q]]), (0, lambda q: att_st[q]),
                             (-1, lambda q: [tail[q], post[q]])):
                if known is not None:
                    b = known + off
                    if not 0 <= b < B:
                        continue
                    out += [(s, b) for s in sts(b % 2)]
                else:
                    reg, d = i
                    out += [(s, (reg, d + off)) for s in sts((d + off) % 2)]
            return out

        s_w, s_c, s_setup, s_zero = (ctx.enter_context(nc.semaphore(n)) for n in
                                     ("w_in", "const_in", "setup_dve", "zero_out"))
        s_sp = ctx.enter_context(nc.semaphore("setup_pool"))
        s_sa = ctx.enter_context(nc.semaphore("setup_act"))
        N_W, SETUP = 11, 2 + 3 * DH + 8

        def run(e, eng):
            for i in (-2, -1, 0, 1):
                issue(e, eng, parts(None, i), ev)
            with e.Fori(2, B - 3, 2) as r:
                bases = {}
                for d in (0, 1):
                    issue(e, eng, parts((r, d), None), ev, bases)
            for i in (B - 2, B - 1, B):
                issue(e, eng, parts(None, i), ev)

        block = ctx.enter_context(nc.Block())

        @block.sync
        def _(e):
            e.dma_start(cst[:], T["consts"][:, 0:NCONST, :]).then_inc(s_c, 16)
            e.dma_start(expo, T["consts"][:, C_EXPO:C_EXPO + 2, :]).then_inc(s_c, 16)
            for dst, src in ((iota[:], T["iota"]), (decay[:], T["decay"]), (lalpha[:], T["log_alpha"])):
                e.dma_start(dst, src).then_inc(s_c, 16)
            for dst, src in ((wq, "Wq"), (wkv[:, :, 0:HD], "Wk"), (wkv[:, :, HD:2 * HD], "Wv"), (wo, "Wo"),
                             (ww, "WwT"), (wr, "WrT"), (wg, "Wg")):
                e.dma_start(dst[:] if src not in ("Wk", "Wv") else dst,
                            T[src].rearrange("(c p) n -> p c n", p=P)).then_inc(s_w, 16)
            e.dma_start(bq[:], T["bq"]).then_inc(s_w, 16)
            e.dma_start(bo[:], T["bo"]).then_inc(s_w, 16)
            e.dma_start(bkv[0:HD, :], T["bk"]).then_inc(s_w, 16)
            e.dma_start(bkv[HD:2 * HD, :], T["bv"]).then_inc(s_w, 16)
            e.wait_ge(s_sp, 1)
            e.dma_start(T["disp"].rearrange("(n p) d -> p n d", p=P),
                        xn3[:].unsqueeze(1).to_broadcast([P, ROWS // P + 1, D])).then_inc(s_zero, 16)
            run(e, "sp")
            for l in all_lanes:
                if l.per:
                    e.wait_ge(l.sem, B * l.per)

        @block.gpsimd
        def _(e):
            e.memset(xn3[:], 0.0).then_inc(s_sp, 1)
            e.memset(mhalf[:], -0.5).then_inc(s_sp, 1)
            e.memset(eps[:], EPS).then_inc(s_sp, 1)
            e.memset(before[:], 0.0).then_inc(s_sp, 1)
            e.memset(rkT[:, :, 0:1], 0.0).then_inc(s_sp, 1)
            e.wait_ge(s_sp, 5)
            e.wait_ge(s_w, 16 * N_W)
            e.wait_ge(s_c, 80)
            e.wait_ge(s_zero, 16)
            e.wait_ge(s_setup, SETUP)
            run(e, "pool")

        @block.scalar
        def _(e):
            e.wait_ge(s_c, 80)
            e.activation(logg[:], decay[:], ACT.Exp, scale=-1.0).then_inc(s_sa, 1)
            e.activation(alpha[:], lalpha[:], ACT.Exp).then_inc(s_sa, 1)
            e.wait_ge(s_setup, 2)
            e.activation(logg[:], logg[:], ACT.Ln).then_inc(s_sa, 1)
            e.wait_ge(s_sa, 3)
            e.activation(gamma[:], logg[:], ACT.Exp).then_inc(s_sa, 1)
            for n, dst in enumerate((decT, decI)):
                for h in range(DH):
                    e.activation(dst[:, h, :], expo[:, n, :], ACT.Exp, scale=logg[:, h:h + 1]).then_inc(s_sa, 1)
            e.wait_ge(s_setup, SETUP)
            e.wait_ge(s_w, 16 * N_W)
            run(e, "act")

        @block.vector
        def _(e):
            n = [0]

            def own(ins):
                n[0] += 1
                ins.then_inc(s_setup, 1)
                e.wait_ge(s_setup, n[0])
            e.wait_ge(s_sa, 2)
            own(e.tensor_scalar(logg[:], logg[:], 1.0, None, ALU.add))
            own(e.reciprocal(logg[:], logg[:]))
            e.wait_ge(s_sa, 4 + 2 * DH)
            for h in range(DH):
                own(e.tensor_tensor(decT[:, h, :], decT[:, h, :], cst[:, C_UPPER, :], ALU.mult))
                own(e.scalar_tensor_tensor(decI[:, h, :], decI[:, h, :], alpha[:, h:h + 1], cst[:, C_UPPER, :],
                                           ALU.mult, ALU.mult))
            for h in range(DH):
                own(e.tensor_scalar(dec1[:, h, :], cst[:, C_PAIR, :], gamma[:, h:h + 1], None, ALU.mult))
            e.wait_ge(s_w, 16 * N_W)
            own(e.tensor_copy(wkv2[:, :, 0:2 * HD], wkv))
            own(e.tensor_tensor(wkv2[:, :, 2 * HD:4 * HD], wkv, wkv2[:, :, 0:2 * HD].bitcast(F32), ALU.subtract))
            for q in (0, 1):
                own(e.memset(v3[q][:, :, 2 * HD:2 * HD + 1].bitcast(F32), 1.0))
            own(e.memset(kvs[2 * HD:P, :], 0.0))
            for q in (0, 1):
                own(e.memset(kT[q][3 * HD:3 * HD + 1, :].bitcast(F32), 1.0))
            own(e.tensor_scalar(bq[:], bq[:], SCALE, None, ALU.mult))
            assert n[0] == SETUP
            e.wait_ge(s_sp, 5)
            run(e, "dve")

        @block.tensor
        def _(e):
            e.wait_ge(s_setup, SETUP)
            e.wait_ge(s_w, 16 * N_W)
            e.wait_ge(s_sp, 5)
            run(e, "pe")


def second_pipeline(nc, T):
    with ExitStack() as ctx:
        def sb(name, shape, dt=F32):
            return ctx.enter_context(nc.sbuf_tensor(name, shape, dt))

        def lane(name):
            return Lane(ctx.enter_context(nc.semaphore(name)))

        bank = [ctx.enter_context(nc.psum_tensor(f"ebank{i}", [P, 512], F32)) for i in range(8)]
        T_BANK, H_BANK, Y_BANK = bank[0], bank[1:5], bank[5:7]
        w1 = [sb(f"w1{i}", [P, DC, F]) for i in range(2)]
        w2 = [sb(f"w2{i}", [P, FT, D]) for i in range(2)]
        dis = [sb(f"dis{i}", [P, D]) for i in range(2)]
        dT = [sb(f"dT{i}", [P, DC, P]) for i in range(2)]
        hT = [sb(f"hT{i}", [P, 4 * P]) for i in range(4)]
        eo = [sb(f"eo{i}", [P, D]) for i in range(2)]
        ident = sb("eident", [P, P])
        lanes = {("expert", e): lane(f"expert_{e}") for e in ("pe", "dve", "act", "pool")}
        L_w1 = [[lane(f"w1_in{i}{j}") for j in range(2)] for i in range(2)]
        L_w2 = [[lane(f"w2_in{i}{j}") for j in range(2)] for i in range(2)]
        L_d, L_y = [lane(f"rows_in{i}") for i in range(2)], [lane(f"rows_out{i}") for i in range(2)]
        s_id = ctx.enter_context(nc.semaphore("ident_in"))
        ev, load, comp = {}, {}, {}
        for q in (0, 1):
            names = ev
            ld = Stage("load", lanes, names)
            cp = Stage("expert", lanes, names if q == 0 else {})
            if q:
                for l in lanes.values():
                    l.per, l.n = l.n, 0
            H = F // 2
            ld.at(0.0)
            ld.dma("sp", lambda e, b, q=q: e.dma_start(dis[q][:], T["disp"].rearrange("(n p) d -> n p d", p=P)[
                bass.ds(b, 1)].rearrange("o p d -> p (o d)")), f"rows{q}", L_d[q], after=[("dTp", 2)])
            for j in range(2):
                ld.at(1.0 + j)
                ld.dma("sp", lambda e, b, q=q, j=j: e.dma_start(
                    w1[q][:, :, j * H:(j + 1) * H], T["w1"][bass.ds(b, 1)].rearrange(
                        "o (c p) f -> p (o c) f", p=P)[:, :, j * H:(j + 1) * H]), f"w1{q}{j}", L_w1[q][j],
                    after=[(f"H{2 * j + 1}", 2)])
            for j in range(2):
                ld.at(3.0 + j)
                ld.dma("sp", lambda e, b, q=q, j=j: e.dma_start(
                    w2[q][:, 8 * j:8 * j + 8, :], T["w2"][bass.ds(b, 1)].rearrange(
                        "o (h c p) m -> h p (o c) m", p=P, h=2)[j]), f"w2{q}{j}", L_w2[q][j],
                    after=[(f"Y{2 * j + 1}", 2)])

            def turn(e, b, q=q):
                for c in range(DC):
                    i = e.transpose(T_BANK[:, c * P:(c + 1) * P], dis[q][:, c * P:(c + 1) * P], ident[:])
                return i
            cp.at(0.0)
            cp.step("pe", turn, "dTp", [f"rows{q}", ("dT", 1)])
            cp.step("dve", lambda e, b, q=q: e.tensor_copy(dT[q][:].rearrange("p c t -> p (c t)"), T_BANK[:]), "dT",
                    ["dTp", ("H3", 2)])

            def up(e, b, g, q):
                for f in range(4):
                    for c in range(DC):
                        i = e.matmul(H_BANK[g][:, f * P:(f + 1) * P],
                                     w1[q][:, c, (4 * g + f) * P:(4 * g + f + 1) * P], dT[q][:, c, :],
                                     start=c == 0, stop=c == DC - 1)
                return i

            def down(e, b, g, q):
                for f in range(4):
                    i = e.matmul(Y_BANK[q][:], hT[g][:, f * P:(f + 1) * P], w2[q][:, 4 * g + f, :],
                                 start=g == 0 and f == 0, stop=g == 3 and f == 3)
                return i

            for g in range(4):
                cp.at(1.0 + g)
                cp.step("pe", lambda e, b, g=g, q=q: up(e, b, g, q), f"H{g}",
                        [f"w1{q}{g // 2}", "dT", (f"relu{g}", 1)])
                if g % 2:
                    cp.step("act", lambda e, b, g=g: e.activation(hT[g][:], H_BANK[g][:], ACT.Relu), f"relu{g}",
                            [f"H{g}", (f"Y{g}", 1)])
                else:
                    cp.step("dve", lambda e, b, g=g: e.tensor_scalar(hT[g][:], H_BANK[g][:], 0.0, None, ALU.max),
                            f"relu{g}", [f"H{g}", (f"Y{g}", 1)])
                if g:
                    cp.step("pe", lambda e, b, g=g - 1, q=q: down(e, b, g, q), f"Y{g - 1}",
                            [f"relu{g - 1}", f"w2{q}{(g - 1) // 2}"] + ([("eo", 2)] if g == 1 else []))
            cp.at(5.0)
            cp.step("pe", lambda e, b, q=q: down(e, b, 3, q), "Y3", ["relu3", f"w2{q}1"])
            cp.step("act", lambda e, b, q=q: e.copy(eo[q][:], Y_BANK[q][:]), "eo", ["Y3", (f"out{q}", 2)])
            cp.dma("sp", lambda e, b, q=q: e.dma_start(T["eo"].rearrange("(n p) d -> n p d", p=P)[
                bass.ds(b, 1)].rearrange("o p d -> p (o d)"), eo[q][:]), f"out{q}", L_y[q], after=["eo"])
            for n, v in cp.events.items():
                ev.setdefault(n, v)
            load[q], comp[q] = ld, cp
        for (_, l) in lanes.items():
            assert l.per == l.n
        halves = L_d + L_y + [l for x in L_w1 + L_w2 for l in x]
        for l in halves:
            l.per = 8
        for n, (l, k) in list(ev.items()):
            if l in halves:
                ev[n] = (l, 16 - 8 * int(n[-1 if l in L_d + L_y else -2]))

        def run(e, eng):
            def parts(r, i):
                b = [(load, i + 1), (comp, i)]
                if r is None:
                    return [(s[n % 2], n) for s, n in b if 0 <= n < E]
                return [(s[n % 2], (r, n)) for s, n in b]
            for i in (-1, 0, 1):
                issue(e, eng, parts(None, i), ev)
            with e.Fori(2, E - 3, 2) as r:
                bases = {}
                for d in (0, 1):
                    issue(e, eng, parts(r, d), ev, bases)
            for i in (E - 2, E - 1):
                issue(e, eng, parts(None, i), ev)

        block = ctx.enter_context(nc.Block())

        @block.sync
        def _(e):
            e.dma_start(ident[:], T["consts"][:, C_IDENT, :]).then_inc(s_id, 16)
            run(e, "sp")
            for l in list(lanes.values()) + halves:
                if l.per:
                    e.wait_ge(l.sem, E * l.per)

        @block.tensor
        def _(e):
            e.wait_ge(s_id, 16)
            run(e, "pe")

        @block.scalar
        def _(e):
            run(e, "act")

        @block.vector
        def _(e):
            run(e, "dve")


def last_part(nc, T, keep):
    N = 4
    with ExitStack() as ctx:
        gidx_all, gate_all = keep
        rows = [ctx.enter_context(nc.sbuf_tensor(f"rows{i}", [P, D], F32)) for i in range(N)]
        res = [ctx.enter_context(nc.sbuf_tensor(f"res{i}", [P, D], F32)) for i in range(N)]
        index = ctx.enter_context(nc.sbuf_tensor("index", [P, B], U32))
        s_rows, s_res, s_out = ([ctx.enter_context(nc.semaphore(f"{n}{i}")) for i in range(N)]
                                for n in ("s_rows", "s_res", "s_out"))
        s_sum, s_index = ctx.enter_context(nc.semaphore("s_sum")), ctx.enter_context(nc.semaphore("s_index"))
        block = ctx.enter_context(nc.Block())

        @block.gpsimd
        def _(e):
            e.wait_ge(s_index, 1)
            for b in range(B):
                if b >= N:
                    e.wait_ge(s_sum, b - N + 1)
                e.indirect_dma_start(out=rows[b % N][:], out_offset=None, in_=T["eo"][:],
                                     in_offset=bass.IndirectOffsetOnAxis(ap=index[:, b:b + 1], axis=0)
                                     ).then_inc(s_rows[b % N], 16)

        @block.sync
        def _(e):
            for b in range(B + N - 1):
                if b < B:
                    if b >= N:
                        e.wait_ge(s_out[b % N], 16 * (b // N))
                    e.dma_start(res[b % N][:], T["x2"][b]).then_inc(s_res[b % N], 16)
                if b >= N - 1:
                    o = b - N + 1
                    e.wait_ge(s_sum, o + 1)
                    e.dma_start(T["out"][o], res[o % N][:]).then_inc(s_out[o % N], 16)
            for i in range(N):
                e.wait_ge(s_out[i], 16 * (B // N))

        @block.vector
        def _(e):
            e.tensor_copy(index[:], gidx_all[:]).then_inc(s_index, 1)
            for b in range(B):
                e.wait_ge(s_rows[b % N], 16 * (b // N + 1))
                e.wait_ge(s_res[b % N], 16 * (b // N + 1))
                e.scalar_tensor_tensor(res[b % N][:], rows[b % N][:], gate_all[:, b:b + 1], res[b % N][:],
                                       ALU.mult, ALU.add).then_inc(s_sum, 1)


def program(nc, T):
    with ExitStack() as ctx:
        keep = [ctx.enter_context(nc.sbuf_tensor(n, [P, B], F32)) for n in ("gidx_all", "gate_all")]
        first_pipeline(nc, T, keep)
        nc.all_engine_barrier()
        second_pipeline(nc, T)
        nc.all_engine_barrier()
        last_part(nc, T, keep)


def tables():
    c = np.zeros((P, NCONST + 2, P), np.float32)
    r, q = np.arange(P)[:, None], np.arange(P)[None, :]
    c[:, C_IDENT] = r == q
    same = r // CH == q // CH
    c[:, C_EXPO] = np.where(r < q, np.where(same, q - r, CH - 1 - r), 0)
    c[:, C_EXPO_I] = np.where(r < q, np.where(same, q - r, q - 1 - r), 0)
    c[:, C_UPPER] = r < q
    c[:, C_PAIR] = -1.0 * ((r % 2 == 1) & (q == r - 1))
    c[:, C_PAIR_T] = -1.0 * ((q % 2 == 1) & (r == q - 1))
    c[:, C_ONES] = 1.0
    c[:, C_DUMP] = ROWS + r
    for n in range(6):
        s = 2 << n
        c[:, C_LEVEL + n] = (r // (2 * s) == q // (2 * s)) & (r % (2 * s) >= s) & (q % (2 * s) < s)
    return c


def kernel(**inputs):
    from concourse import bacc
    from concourse.bass_utils import run_bass_kernel_spmd

    nc = bacc.Bacc("TRN2", target_bir_lowering=False, num_devices=1)
    g = {k: np.asarray(v) for k, v in inputs.items()}

    def rows(v):
        return np.ascontiguousarray(np.broadcast_to(v[None, :], (P, v.shape[0])))
    arrays = {
        "x": g["x"], "ctx": g["ctx_1024"], "Wq": g["L0_xattn_Wq"], "Wk": g["L0_xattn_Wk"],
        "Wv": g["L0_xattn_Wv"], "Wo": g["L0_xattn_Wo"], "bq": rows(g["L0_xattn_bq"]),
        "bk": g["L0_xattn_bk"].reshape(HD, 1), "bv": g["L0_xattn_bv"].reshape(HD, 1), "bo": rows(g["L0_xattn_bo"]),
        "WwT": np.ascontiguousarray(g["L0_attn_Ww"].T), "WrT": np.ascontiguousarray(g["L0_attn_Wr"].T),
        "decay": rows(g["L0_attn_decay"]), "log_alpha": rows(g["L0_attn_log_alpha"]), "Wg": g["L0_ffn_Wg"],
        "w1": g["L0_ffn_w1"], "w2": g["L0_ffn_w2"], "consts": tables(),
        "iota": rows(np.arange(E, dtype=np.float32) - E),
    }
    T = {k: nc.dram_tensor(f"in_{k}", v.shape, F32, kind="ExternalInput").ap() for k, v in arrays.items()}
    T["out"] = nc.dram_tensor("out", (B, P, D), F32, kind="ExternalOutput").ap()
    T["x2"] = nc.dram_tensor("x2_scratch", (B, P, D), F32, kind="Internal").ap()
    T["disp"] = nc.dram_tensor("dispatched", (ROWS + P, D), F32, kind="Internal").ap()
    T["eo"] = nc.dram_tensor("expert_rows", (ROWS, D), F32, kind="Internal").ap()
    program(nc, T)
    r = run_bass_kernel_spmd(nc, [{f"in_{k}": v for k, v in arrays.items()}], core_ids=[0])
    return r.results[0]["out"]
```

```python
from contextlib import ExitStack

import numpy as np
import concourse.bass as bass
from concourse import mybir

F32, F32R, U32 = mybir.dt.float32, mybir.dt.float32r, mybir.dt.uint32
ALU, ACT, AX = mybir.AluOpType, mybir.ActivationFunctionType, mybir.AxisListType

P = 128
B, S, D = 16, 2048, 512
NH, HD = 16, 32
DC = D // P
KB = S // P
HG = NH // 4
DH = 4
CH = 64
E, F = 16, 2048
FT = F // P
CAP = (B * P + E - 1) // E
ROWS = E * CAP
EPS = 1e-5
SCALE = float(HD) ** -0.5
ROUTE = 2 * D + 2
C_IDENT, C_UPPER, C_PAIR, C_ONES, C_DUMP, C_LEVEL = range(6)
NCONST = C_LEVEL + 6
C_EXPO, C_EXPO_I = NCONST, NCONST + 1
NF, NHI, NL = 2, 4, 4
AT = {
    "norm": 2.04, "q_proj": 5.42, "q_split": 7.73, "q_turn": 8.57, "q_copy": 0.14,
    "turn_first": 13.3, "turn_pace": 2.25, "cxh": 0.4, "cxl": 0.7,
    "kv0": 1.26, "kv1": 1.45, "kvlow": 2.0, "kvs": 2.2, "kh": 2.2, "kl": 2.21,
    "v_turn": 0.77, "vh": 0.29, "vl": 0.57,
    "max0": 51.1, "max0_pace": 0.64, "max": 0.79, "max_pace": 0.76, "max_after": 0.6,
    "exp": 0.24, "low": 0.43, "weigh": 2.29,
    "os": 0.1, "o_turn": 0.76, "normalise": 1.0,
    "post": 3.0, "post_pe": 0.45, "post_gap": 0.8, "double_gap": 0.8, "route_gap": 0.8, "post_end": 63.0,
    "rows_turn": 4.0, "w2_split": 0.5, "relu": 0.5,
}
LOW_ON_DVE = (2, 63)
UNITS = HG * KB


class Lane:

    def __init__(self, sem):
        self.sem, self.per, self.n = sem, None, 0


class Stage:

    def __init__(self, name, lanes, events, clock=0.0):
        self.name, self.lanes, self.events, self.t, self.steps = name, lanes, events, clock, []

    def at(self, t):
        assert t >= self.t - 1e-9, (self.name, self.t, t)
        self.t = t

    def step(self, eng, fn, name=None, after=(), lane=None, by=1):
        if name is not None and lane is None:
            lane = self.lanes[(self.name, eng)]
        if name is not None:
            lane.n += by
            assert name not in self.events, name
            self.events[name] = (lane, lane.n)
        self.steps.append((self.t, eng, fn, name is not None and (lane, by), tuple(after)))

    def stretch(self, end):
        self.steps = [(s[0] * end / self.t,) + s[1:] for s in self.steps]

    def dma(self, eng, fn, name, lane, after=()):
        self.step(eng, fn, name, after, lane, 16)


def issue(e, eng, parts, events, bases=None, now={}):
    merged = sorted(((s[0], n, j, s, b) for n, (st, b) in enumerate(parts)
                     for j, s in enumerate(st.steps)), key=lambda m: m[:3])
    for _, _, _, (_, on, fn, mark, after), b in merged:
        if on != eng:
            continue
        need = {}
        for a in after:
            name, ago = a if isinstance(a, tuple) else (a, 0)
            lane, k = events[name] if ago or name not in now else now[name]
            if not isinstance(b, int) or b >= ago:
                off = b if isinstance(b, int) else b[1]
                need[lane] = max(need.get(lane, -10**6), (off - ago) * lane.per + k)
        for lane, n in need.items():
            if not isinstance(b, int):
                if lane not in bases:
                    bases[lane] = e.snap(b[0] * lane.per)
                n = bases[lane] + n
            e.wait_ge(lane.sem, n)
        ins = fn(e, b if isinstance(b, int) else b[0] + b[1])
        if mark:
            ins.then_inc(mark[0].sem, mark[1])


def load_w1(e, T, dst, expert, half):
    cols = slice(half * (F // 2), (half + 1) * (F // 2))
    return e.dma_start(dst[:, :, cols], T["w1"][bass.ds(expert, 1)].rearrange(
        "o (c p) f -> p (o c) f", p=P)[:, :, cols])


def first_pipeline(nc, T, w1_first, w1_sems):
    with ExitStack() as ctx:
        def sb(name, shape, dt=F32):
            return ctx.enter_context(nc.sbuf_tensor(name, shape, dt))

        def lane(name):
            return Lane(ctx.enter_context(nc.semaphore(name)))

        bank = [ctx.enter_context(nc.psum_tensor(f"bank{i}", [P, 512], F32)) for i in range(8)]
        A_BANK, B_BANK, PV_BANK, T_BANK, KV_BANK, POST = bank[0:2], bank[2:4], bank[4], bank[5], bank[6], bank[7]

        cst = sb("cst", [P, NCONST, P])
        ident = cst[:, C_IDENT, :]
        iota = sb("iota", [P, E])
        wq, wo, ww, wr = (sb(n, [P, DC, D]) for n in ("wq", "wo", "ww", "wr"))
        wkv2 = sb("wkv2", [P, DC, 4 * HD], F32R)
        wg = sb("wg", [P, DC, E])
        bq, bo, bkv = sb("bq", [P, D]), sb("bo", [P, D]), sb("bkv", [2 * HD, 1])
        decay, lalpha = sb("decay", [P, DH]), sb("lalpha", [P, DH])
        logg, alpha = sb("logg", [P, DH]), sb("alpha", [P, DH])
        decT, decI = (sb(n, [P, DH, P]) for n in ("decT", "decI"))
        mhalf, eps = sb("mhalf", [P, DH]), sb("eps", [P, 1])
        pad_dve, pad_pool = sb("pad_dve", [P, 1]), sb("pad_pool", [P, 1])
        cx = [w1_first[:, c, :].rearrange("p (k d) -> p k d", k=4) for c in range(4)]
        cxh, cxl = sb("cxh", [P, DC, 512], F32R), sb("cxl", [P, DC, 512], F32R)
        kvlow, kvs = sb("kvlow", [2 * HD, 512]), sb("kvs", [P, 512])
        v3 = [sb(f"v3{i}", [P, KB, 2 * HD + 1], F32R) for i in range(2)]
        kT = [sb(f"kT{i}", [P, S], F32R) for i in range(2)]
        qT = [sb(f"qT{i}", [P, NH * P], F32R) for i in range(2)]
        xin, xnT, qf = sb("xin", [P, D]), sb("xnT", [P, DC, P]), sb("qf", [P, D])
        xn = xin
        q3 = sb("q3", [P, NH, 3 * HD])
        st1, mv1, rs1 = sb("st1", [P, 6]), sb("mv1", [P, 2]), sb("rs1", [P, 2])
        pf = [sb(f"pf{i}", [P, 512]) for i in range(NF)]
        ph = [sb(f"ph{i}", [P, 512], F32R) for i in range(NHI)]
        pl = [sb(f"pl{i}", [P, 512], F32R) for i in range(NL)]
        oS, oN, oSum = sb("oS", [2 * HD + 1, 512]), sb("oN", [P, 4, 2 * HD + 1]), sb("oSum", [P, 4, HD])
        mpart = [sb(f"mpart{i}", [P, 16]) for i in range(2)]
        mneg = sb("mneg", [P, 4])
        mrow = [sb(f"mrow{i}", [4, P], F32R) for i in range(2)]
        rsum = sb("rsum", [P, 4])
        att = [sb(f"att{i}", [P, D]) for i in range(2)]
        xr, x1, xn2, x12, rk, V, Y, turned = (
            sb(n, [P, D]) for n in ("xr", "x1", "xn2", "x12", "rk", "V", "Y", "turned"))
        route = sb("route", [P, ROUTE])
        xn3, x2 = route[:, 0:D], route[:, D:2 * D]
        token = sb("token", [P, 1])
        XT, MT, X, IT, Vn = xr, x1, xn2, rk, Y
        oT1 = xn2T = oT2 = xn3T = turned
        wkv = V[:, 0:2 * HD * DC].rearrange("p (c n) -> p c n", c=DC)
        expo = Y[:, 0:2 * P].rearrange("p (k t) -> p k t", k=2)
        rkT = sb("rkT", [P, DH, P + 1])
        st2, mv2, rs2 = sb("st2", [P, 6]), sb("mv2", [P, 2]), sb("rs2", [P, 2])
        st3, mv3, rs3 = sb("st3", [P, 6]), sb("mv3", [P, 2]), sb("rs3", [P, 2])
        ss, rn = sb("ss", [P, DH]), sb("rn", [P, DH])
        lg, eg, oh, oh2 = (sb(n, [P, E]) for n in ("lg", "eg", "oh", "oh2"))
        before = sb("before", [P, E])
        sc = sb("sc", [P, 12])
        sidx = sb("sidx", [P, 1], U32)

        lanes = {(s, e): lane(f"{s}_{e}") for s in ("prep", "attn", "tail", "max", "post")
                 for e in ("pe", "dve", "act", "pool")}
        L_ctx = [lane(f"ctx_in{c}") for c in range(4)]
        L_x, L_xr, L_x2, L_scat = lane("x_in"), lane("xr_in"), lane("x2_out"), lane("scatter_out")
        L_mrow = [lane(f"mrow_dma{g}") for g in range(HG)]
        ev = {}

        def aggregate(e, out, in_):
            e.memset(pad_dve[:], 0.0)
            return e.bn_aggr(out, in_)

        def scatter(e):
            e.tensor_tensor(pad_pool[:], mhalf[:, 0:1], mhalf[:, 0:1], ALU.mult)
            return e.indirect_dma_start(
                out=T["disp"][:], out_offset=bass.IndirectOffsetOnAxis(ap=sidx[:, 0:1], axis=0), in_=route[:],
                in_offset=None)

        def transposes(e, out, src, n=4, m=P):
            for j in range(n):
                i = e.transpose(out[0:m, j * P:(j + 1) * P], src(j), ident)
            return i

        def copy(on, e, out, in_):
            return e.copy(out, in_) if on == "act" else e.tensor_copy(out, in_)

        load = Stage("load", lanes, ev)
        load.at(8.0)
        load.dma("sp", lambda e, b: e.dma_start(xin[:], T["x"][bass.ds(b, 1)].rearrange("o p d -> p (o d)")),
                 "x", L_x, after=[("xnTp", 1)])
        for c in range(4):
            load.at(AT["turn_first"] + AT["turn_pace"] * (4 * c + 3) + 0.5)
            load.dma("sp", lambda e, b, c=c: e.dma_start(cx[c], T["ctx"][bass.ds(b, 1)].rearrange(
                "o (p c k) d -> c p (o k) d", c=4, k=4)[c]), f"ctx{c}", L_ctx[c],
                after=[(f"T{4 * c + 3}", 1)])

        def prep_steps(st, q, banks):
            uses = []

            def turn_bank(reader):
                n = len(uses)
                uses.append(reader)
                return banks[n % len(banks)], uses[n - len(banks)] if n >= len(banks) else ("vl3", 1)

            st.at(0.0)
            st.at(AT["norm"])
            st.step("dve", lambda e, b: e.bn_stats(st1[:], xin[:]), "st1", ["x"])
            st.step("dve", lambda e, b: aggregate(e, mv1[:], st1[:]), "mv1", ["st1"])
            st.step("pool", lambda e, b: e.tensor_tensor(rs1[:, 0:1], mv1[:, 1:2], eps[:, 0:1], ALU.add), "ve1",
                    ["mv1"])
            st.step("pool", lambda e, b: e.tensor_tensor(rs1[:, 1:2], rs1[:, 0:1], mhalf[:, 0:1], ALU.pow), "rs1",
                    ["ve1"])
            st.at(3.5)
            st.step("dve", lambda e, b: e.tensor_scalar(xn[:], xin[:], mv1[:, 0:1], rs1[:, 1:2], ALU.subtract,
                                                        ALU.mult), "xn", ["mv1", "rs1", ("xnTp", 1)])
            st.at(4.5)
            bank, prev = turn_bank("xnT")
            st.step("pe", lambda e, b, bank=bank: transposes(e, bank, lambda j: xn[:, j * P:(j + 1) * P]), "xnTp",
                    ["xn", prev])
            st.at(5.0)
            st.step("act", lambda e, b, bank=bank: e.copy(xnT[:].rearrange("p c t -> p (c t)"), bank[:]), "xnT",
                    ["xnTp"])

            for c in range(DC):
                st.at(AT["q_proj"] + 0.5 * c)
                st.step("pe", lambda e, b, c=c: e.matmul(KV_BANK[:], xnT[:, c, :], wq[:, c, :], start=c == 0,
                                                         stop=c == DC - 1), "Qp" if c == DC - 1 else None,
                        ["xnT", ("kvs3", 1)] if c == 0 else [])
            st.at(AT["q_split"])
            st.step("dve", lambda e, b: e.scalar_tensor_tensor(qf[:], KV_BANK[:], SCALE, bq[:], ALU.mult, ALU.add),
                    "qf", ["Qp", ("qh", 1)])
            q4, qf4 = q3[:], qf[:].rearrange("p (h d) -> p h d", h=NH)
            qh = q4.bitcast(F32R)
            st.step("dve", lambda e, b: e.tensor_copy(qh[:, :, 0:HD], qf4), "qh0", ["qf", ("qTp3", 1)])
            st.step("act", lambda e, b: e.copy(qh[:, :, HD:2 * HD], qf4), "qh", ["qf", ("qTp3", 1)])
            st.step("dve", lambda e, b: e.tensor_tensor(q4[:, :, 2 * HD:3 * HD], qf4, q4[:, :, 0:HD], ALU.subtract),
                    "ql", ["qh0"])
            for g in range(HG):
                st.at(AT["q_turn"] + 0.95 * g)
                bank, prev = turn_bank(f"qT{g}")
                st.step("pe", lambda e, b, g=g, bank=bank: transposes(
                    e, bank, lambda j: q3[:, 4 * g + j, :], 4, 3 * HD),
                        f"qTp{g}", ["qh", "ql", prev])
                st.at(AT["q_turn"] + 0.95 * g + AT["q_copy"])
                on = "act" if g % 2 else "dve"
                st.step(on, lambda e, b, g=g, on=on, bank=bank: copy(
                    on, e, qT[q][0:3 * HD, g * 512:(g + 1) * 512], bank[0:3 * HD, :]),
                        f"qT{g}", [f"qTp{g}", (f"B{UNITS - 1}", 2)])
            def turn_v(st, c, t):
                bank, prev = turn_bank(f"vl{c}")
                vb = bank[:].rearrange("p (k n) -> p k n", k=4)[:, :, HD:2 * HD]
                vk = slice(4 * c, 4 * c + 4)
                st.at(t)
                st.step("pe", lambda e, b: transposes(e, bank, lambda j: kvs[:, j * P:(j + 1) * P]), f"vTp{c}",
                        [f"kvs{c}", prev])
                st.at(t + AT["vh"])
                st.step("act", lambda e, b: e.copy(v3[q][:, vk, 0:HD], vb), f"vh{c}",
                        [f"vTp{c}", (f"PV{UNITS - 1}", 2)])
                st.at(t + AT["vl"])
                st.step("dve", lambda e, b: e.tensor_tensor(
                    v3[q][:, vk, HD:2 * HD], vb, v3[q][:, vk, 0:HD].bitcast(F32), ALU.subtract), f"vl{c}",
                    [f"vh{c}"])

            for k in range(KB):
                t = AT["turn_first"] + AT["turn_pace"] * k
                c, kk = divmod(k, 4)
                cols = slice(kk * P, (kk + 1) * P)
                if kk == 2 and c:
                    turn_v(st, c - 1, t - AT["turn_pace"] + AT["v_turn"])
                st.at(t)
                bank, prev = turn_bank(f"cxl{k}")
                bank3 = bank[:].rearrange("p (c t) -> p c t", c=DC)
                st.step("pe", lambda e, b, c=c, kk=kk, bank=bank: transposes(
                    e, bank, lambda j: cx[c][:, kk, j * P:(j + 1) * P]), f"T{k}", [f"ctx{c}", prev])
                st.at(t + AT["cxh"])
                st.step("act", lambda e, b, cols=cols, bank3=bank3: e.copy(cxh[:, :, cols], bank3), f"cxh{k}",
                        [f"T{k}"] + ([f"KVp{c - 1}" if c else ("KVp3", 1)] if kk == 0 else []))
                st.at(t + AT["cxl"])
                st.step("dve", lambda e, b, cols=cols, bank3=bank3: e.tensor_tensor(
                    cxl[:, :, cols], bank3, cxh[:, :, cols].bitcast(F32), ALU.subtract), f"cxl{k}", [f"cxh{k}"])
                if kk < 3:
                    continue

                def kv_proj(e, b, half):
                    for j in (2 * half, 2 * half + 1):
                        e.matmul(KV_BANK[:], wkv2[:, j, :], cxh[:, j, :], start=j == 0, stop=False)
                        i = e.matmul(KV_BANK[:], wkv2[:, j, :], cxl[:, j, :], start=False, stop=j == DC - 1)
                    return i
                st.at(t + AT["kv0"])
                st.step("pe", lambda e, b: kv_proj(e, b, 0), None, [f"cxl{k}", f"kvs{c - 1}" if c else "qf"])
                st.at(t + AT["kv1"])
                st.step("pe", lambda e, b: kv_proj(e, b, 1), f"KVp{c}")
                st.at(t + AT["kvlow"])
                st.step("act", lambda e, b: e.copy(kvlow[:], KV_BANK[2 * HD:4 * HD, :]), f"kvlow{c}",
                        [f"KVp{c}", f"kvs{c - 1}" if c else ("kvs3", 1)])
                st.at(t + AT["kvs"])
                st.step("dve", lambda e, b: e.scalar_tensor_tensor(
                    kvs[0:2 * HD, :], KV_BANK[0:2 * HD, :], bkv[:, 0:1], kvlow[:], ALU.add, ALU.add), f"kvs{c}",
                    [f"kvlow{c}", f"vTp{c - 1}" if c else ("vTp3", 1), f"kl{c - 1}" if c else ("kl3", 1),
                     f"kh{c - 1}" if c else ("kh3", 1)])
                ks = slice(c * 512, (c + 1) * 512)
                st.at(t + AT["kh"])
                st.step("act", lambda e, b, ks=ks: e.copy(kT[q][0:HD, ks], kvs[0:HD, :]), f"kh{c}",
                        [f"kvs{c}", (f"B{UNITS - 1}", 2)])
                st.step("dve", lambda e, b, ks=ks: e.tensor_copy(kT[q][2 * HD:3 * HD, ks], kvs[0:HD, :]),
                        f"kh2{c}", [f"kvs{c}", (f"B{UNITS - 1}", 2)])
                st.at(t + AT["kl"])
                st.step("dve", lambda e, b, ks=ks: e.tensor_tensor(
                    kT[q][HD:2 * HD, ks], kvs[0:HD, :], kT[q][0:HD, ks].bitcast(F32), ALU.subtract),
                    f"kl{c}", [f"kh{c}"])
            turn_v(st, 3, t + 2.9)
            maxima(st, 0, q, AT["max0"], AT["max0_pace"])

        def maxima(st, g, q, t0, pace):
            for n in range(17):
                use = 17 * g + n
                a = A_BANK[use % 2]
                prev = 17 * g + n - 2
                w = [f"A_free{prev}"] if prev >= 0 else [(f"A_free{prev + 17 * HG}", 1)]
                if n < 16:
                    h, c = divmod(n, 4)
                    st.at(t0 + pace * n)
                    st.step("pe", lambda e, b, h=h, c=c, a=a: e.matmul(
                        a[:], qT[q][0:3 * HD, (4 * g + h) * P:(4 * g + h + 1) * P],
                        kT[q][0:3 * HD, c * 512:(c + 1) * 512], start=True, stop=True), f"A{use}",
                        w + ([f"qT{g}", "kh3", "kh23", "kl3", "qT3"] if n == 0 else []))
                    st.at(t0 + pace * n + AT["max_after"])
                    st.step("dve", lambda e, b, n=n, a=a: e.tensor_reduce(mpart[g % 2][:, n:n + 1], a[:], AX.X,
                                                                          ALU.max), f"A_free{use}", [f"A{use}"])
                else:
                    st.at(t0 + pace * (n - 1) + AT["max_after"])
                    st.step("dve", lambda e, b: e.tensor_reduce(
                        mneg[:], mpart[g % 2][:].rearrange("p (h c) -> p h c", h=4), AX.X, ALU.max, negate=True),
                        f"mneg{g}", [f"A_free{use - 1}", (f"A{17 * g - 1}", 0) if g else (f"A{17 * HG - 1}", 1)])
                    st.at(t0 + pace * (n - 1) + AT["max_after"] + 0.4)
                    st.step("pe", lambda e, b, a=a: e.transpose(a[0:4, 0:P], mneg[:], ident), f"A{use}",
                            w + [f"mneg{g}"])
                    st.at(t0 + pace * (n - 1) + AT["max_after"] + 0.7)
                    st.step("act", lambda e, b, a=a: e.copy(mrow[g % 2][:], a[0:4, 0:P]), f"A_free{use}",
                            [f"A{use}", (f"mrow{g - 2}", 0) if g > 1 else (f"mrow{g + 2}", 1)])
                    st.dma("sp", lambda e, b: e.dma_start(
                        qT[q][3 * HD:3 * HD + 1, g * 512:(g + 1) * 512].bitcast(F32).rearrange(
                            "o (h t) -> o h t", h=4), mrow[g % 2][:].bitcast(F32)),
                           f"mrow{g}", L_mrow[g], after=[f"A_free{use}"])

        def attn_steps(st, tail, q):
            mine = []
            for g in range(HG):
                for k in range(KB):
                    u = g * KB + k

                    def scores(st, g=g, k=k, u=u):
                        w = [f"exp{u - 2}"] if u > 1 else [(f"exp{u - 2 + UNITS}", 1)]
                        if k == 0:
                            w += [f"mrow{g}"]
                        st.step("pe", lambda e, b: e.matmul(
                            B_BANK[u % 2][:], kT[q][0:3 * HD + 1, k * P:(k + 1) * P],
                            qT[q][0:3 * HD + 1, g * 512:(g + 1) * 512], start=True, stop=True), f"B{u}", w)
                    mine.append((u, scores))

                    def expo(st, g=g, k=k, u=u):
                        def free(by, n):
                            return f"{by}{u - n}" if u >= n else (f"{by}{u - n + UNITS}", 1)
                        st.step("act", lambda e, b: e.activation(ph[u % NHI][:], B_BANK[u % 2][:], ACT.Exp),
                                f"exph{u}", [f"B{u}", free("PV", NHI)])
                        st.step("act", lambda e, b: e.activation(pf[u % NF][:], B_BANK[u % 2][:], ACT.Exp),
                                f"exp{u}", [f"B{u}", free("pl", NF)])
                    mine.append((u + AT["exp"], expo))

                    def low(st, g=g, k=k, u=u):
                        def free(by, n):
                            return f"{by}{u - n}" if u >= n else (f"{by}{u - n + UNITS}", 1)
                        on = "dve" if u in LOW_ON_DVE else "pool"
                        st.step(on, lambda e, b: e.tensor_tensor(
                            pl[u % NL][:], pf[u % NF][:], ph[u % NHI][:].bitcast(F32), ALU.subtract),
                            f"pl{u}", [f"exp{u}", free("PV", NL)])
                    mine.append((u + AT["low"], low))

                    def weigh(st, g=g, k=k, u=u):
                        def f(e, b):
                            e.matmul(PV_BANK[0:2 * HD + 1, :], v3[q][:, k, :], ph[u % NHI][:], start=k == 0,
                                     stop=False)
                            return e.matmul(PV_BANK[0:2 * HD + 1, :], v3[q][:, k, :], pl[u % NL][:],
                                            start=False, stop=k == KB - 1)
                        w = [f"pl{u}"]
                        if k == 0:
                            w += [f"oN{g - 1}" if g else (f"oN{HG - 1}", 1), "vl3"]
                        st.step("pe", f, f"PV{u}", w)
                    mine.append((u + AT["weigh"] + (0.7 if k == 0 else 0.2 if k == 1 else 0), weigh))

                def turn(st, g=g):
                    st.step("act", lambda e, b: e.copy(oS[:], PV_BANK[0:2 * HD + 1, :]), f"oS{g}",
                            [f"PV{g * KB + KB - 1}", f"oTp{g - 1}" if g else (f"oTp{HG - 1}", 1)])

                def turn2(st, g=g):
                    def f(e, b):
                        for j in range(4):
                            i = e.transpose(PV_BANK[:, 65 * j:65 * j + 65], oS[:, j * P:(j + 1) * P],
                                            ident[0:2 * HD + 1, 0:2 * HD + 1])
                        return i
                    st.step("pe", f, f"oTp{g}", [f"oS{g}"])

                def normalise(st, g=g):
                    st.step("dve", lambda e, b: e.tensor_copy(oN[:].rearrange("p h n -> p (h n)"),
                                                              PV_BANK[:, 0:4 * 65]), f"oN{g}", [f"oTp{g}"])
                    st.step("dve", lambda e, b: e.reciprocal(rsum[:], oN[:, :, 2 * HD]), f"rsum{g}", [f"oN{g}"])
                    st.step("dve", lambda e, b: e.tensor_tensor(oSum[:], oN[:, :, 0:HD], oN[:, :, HD:2 * HD],
                                                                ALU.add), f"oSum{g}", [f"oN{g}"])
                    st.step("dve", lambda e, b: e.tensor_tensor(
                        att[q][:, g * P:(g + 1) * P].rearrange("p (h n) -> p h n", h=4), oSum[:],
                        rsum[:].unsqueeze(2).to_broadcast([P, 4, HD]), ALU.mult), f"att{g}",
                        [f"rsum{g}", f"oSum{g}"] + ([("oT1p", 2)] if g == 0 else []))
                end = g * KB + KB - 1 + AT["weigh"]
                mine += [(end + AT["os"], turn), (end + AT["o_turn"], turn2), (end + AT["normalise"], normalise)]
            for t, f in sorted(mine, key=lambda m: m[0]):
                to = st if t < UNITS else tail
                to.at(t if t < UNITS else t - UNITS)
                f(to)

        def heads(ap, n=DH):
            return ap.rearrange("p (h t) -> p h t", h=n)

        def post_steps(st, q, banks):
            hop, pace = [AT["post"]], ["post_gap"]

            def pe(fn, name, after=()):
                st.at(hop[0])
                st.step("pe", fn, name, list(after))
                hop[0] += AT["post_pe"]

            def then(eng, fn, name, after=()):
                st.at(max(st.t, hop[0]))
                st.step(eng, fn, name, list(after))

            def gap(n=1.0):
                hop[0] = max(hop[0], st.t) + n * AT[pace[0]]

            def norm(src, dst, stt, mv, rs, tag, dep, war):
                then("dve", lambda e, b: e.bn_stats(stt[:], src), "st" + tag, [dep])
                then("dve", lambda e, b: aggregate(e, mv[:], stt[:]), "mv" + tag, ["st" + tag])
                then("pool", lambda e, b: e.tensor_tensor(rs[:, 0:1], mv[:, 1:2], eps[:, 0:1], ALU.add), "ve" + tag,
                     ["mv" + tag])
                then("pool", lambda e, b: e.tensor_tensor(rs[:, 1:2], rs[:, 0:1], mhalf[:, 0:1], ALU.pow),
                     "rs" + tag, ["ve" + tag])
                gap(0.6)
                then("dve", lambda e, b: e.tensor_scalar(dst, src, mv[:, 0:1], rs[:, 1:2], ALU.subtract,
                                                         ALU.mult), "xn" + tag, ["mv" + tag, "rs" + tag] + war)
                gap(0.6)

            def project(name, lhs, w, after):
                for c in range(DC):
                    pe(lambda e, b, c=c: e.matmul(POST[:], lhs[:, c * P:(c + 1) * P], w[:, c, :], start=c == 0,
                                                  stop=c == DC - 1), name if c == DC - 1 else None,
                       after if c == 0 else [])

            def per_head(name, lhs, rhs, after):
                def f(e, b):
                    for h in range(DH):
                        i = e.matmul(POST[:, h * P:(h + 1) * P], lhs(h), rhs(h), start=True, stop=True)
                    return i
                pe(f, name, after)

            def cut(t):
                return lambda h: t[:, h * P:(h + 1) * P]

            st.at(0.0)
            st.dma("sp", lambda e, b: e.dma_start(xr[:], T["x"][bass.ds(b, 1)].rearrange("o p d -> p (o d)")),
                   "xr", L_xr, after=[("Vnp", 1)])
            st.at(2.0)
            st.step("pool", lambda e, b: e.tensor_tensor(xr[:], xr[:], bo[:], ALU.add), "xb", ["xr"])
            pe(lambda e, b: transposes(e, POST, cut(att[q])), "oT1p", ["att3", ("lg", 1)])
            then("act", lambda e, b: e.copy(oT1[:], POST[:]), "oT1", ["oT1p"])
            gap()
            project("x1p", oT1, wo, ["oT1"])
            then("dve", lambda e, b: e.tensor_tensor(x1[:], POST[:], xr[:], ALU.add), "x1", ["x1p", "xb"])
            norm(x1[:], xn2[:], st2, mv2, rs2, "2", "x1", [])
            then("pool", lambda e, b: e.tensor_tensor(x12[:], x1[:], xn2[:], ALU.add), "x12", ["xn2"])
            pe(lambda e, b: transposes(e, POST, cut(xn2)), "xn2Tp", ["xn2"])
            then("act", lambda e, b: e.copy(xn2T[:], POST[:]), "xn2T", ["xn2Tp"])
            then("dve", lambda e, b: e.tensor_tensor(rk[:], xn2[:], xn2[:], ALU.mult), "sq", ["xn2"])
            then("dve", lambda e, b: e.tensor_reduce(ss[:], heads(rk[:]), AX.X, ALU.add), "ss", ["sq"])
            then("dve", lambda e, b: e.tensor_scalar(rn[:], ss[:], 1e-24, None, ALU.max), "ssm", ["ss"])
            then("pool", lambda e, b: e.tensor_tensor(rn[:], rn[:], mhalf[:], ALU.pow), "rn", ["ssm"])
            gap(0.5)
            then("dve", lambda e, b: e.tensor_tensor(heads(rk[:]), heads(xn2[:]),
                                                     rn[:].unsqueeze(2).to_broadcast([P, DH, P]), ALU.mult),
                 "rk", ["rn", "ss"])
            gap(0.3)
            project("Vp", xn2T, ww, ["xn2T"])
            then("act", lambda e, b: e.copy(V[:], POST[:]), "V", ["Vp"])
            gap()
            pe(lambda e, b: transposes(e, POST, cut(rk)), "rkTp", ["rk", "V"])
            then("act", lambda e, b: e.copy(rkT[:, :, 1:P + 1], heads(POST[:])), "rkT", ["rkTp"])
            gap()
            idb = ident.unsqueeze(1).to_broadcast([P, DH, P])
            then("pool", lambda e, b: e.tensor_tensor(heads(MT[:])[:, :, 0:1], rkT[:, :, 0:1], rkT[:, :, 0:1],
                                                      ALU.mult), "MT0", ["x12"])
            per_head("Ip", lambda h: rkT[:, h, 0:P], lambda h: rkT[:, h, 1:P + 1], ["rkT"])
            then("dve", lambda e, b: e.tensor_tensor(heads(MT[:])[:, :, 1:P], heads(POST[:])[:, :, 0:P - 1],
                                                     decT[:, :, 1:P], ALU.mult), "MT", ["Ip", "x12"])
            then("dve", lambda e, b: e.tensor_tensor(IT[:], POST[:], decI[:].rearrange("p h t -> p (h t)"),
                                                     ALU.mult), "IT", ["Ip"])
            then("dve", lambda e, b: e.tensor_tensor(
                heads(XT[:]), heads(MT[:]), cst[:, C_PAIR, :].unsqueeze(1).to_broadcast([P, DH, P]), ALU.mult),
                "XT1a", ["MT", "MT0"])
            then("pool", lambda e, b: e.tensor_tensor(heads(XT[:]), heads(XT[:]), idb, ALU.add), "XT1", ["XT1a"])
            gap(1.4)
            pe(lambda e, b: transposes(e, POST, cut(XT)), "Xp1", ["XT1", "IT"])
            then("act", lambda e, b: e.copy(X[:], POST[:]), "X1", ["Xp1"])
            gap()
            pace[0] = "double_gap"
            n = DH // len(banks)
            parts = [(f"_{i}" if i else "", bank, range(i * n, (i + 1) * n), slice(i * n * P, (i + 1) * n * P))
                     for i, bank in enumerate(banks)]

            def products(name, tag, bank, hs, lhs, rhs, after):
                def f(e, b):
                    for h in hs:
                        i = e.matmul(bank[:, h * P:(h + 1) * P], lhs(h), rhs(h), start=True, stop=True)
                    return i
                pe(f, name + tag, after)
            for lv in range(6):
                s, prev = 2 << lv, 1 << lv
                for tag, bank, hs, cols in parts:
                    products(f"Yp{s}", tag, bank, hs, cut(MT), cut(X), ["MT", f"X{prev}{tag}" if lv else "X1"])
                    then("dve", lambda e, b, lv=lv, bank=bank, cols=cols: e.tensor_tensor(
                        heads(Y[:, cols], n), heads(bank[:, cols], n),
                        cst[:, C_LEVEL + lv, :].unsqueeze(1).to_broadcast([P, n, P]), ALU.mult), f"Y{s}{tag}",
                        [f"Yp{s}{tag}"])
                gap()
                for tag, bank, hs, cols in parts:
                    products(f"ZTp{s}", tag, bank, hs, cut(Y), cut(XT),
                             [f"Y{s}{tag}", f"XT{prev}{tag}" if lv else "XT1"])
                    then("dve", lambda e, b, bank=bank, cols=cols: e.tensor_tensor(
                        XT[:, cols], XT[:, cols], bank[:, cols], ALU.subtract), f"XT{s}{tag}", [f"ZTp{s}{tag}"])
                gap()
                if s == CH:
                    continue
                for tag, bank, hs, cols in parts:
                    def turn(e, b, bank=bank, hs=hs):
                        for h in hs:
                            i = e.transpose(bank[:, h * P:(h + 1) * P], cut(XT)(h), ident)
                        return i
                    pe(turn, f"Xp{s}{tag}", [f"XT{s}{tag}"])
                    then("act", lambda e, b, bank=bank, cols=cols: e.copy(X[:, cols], bank[:, cols]), f"X{s}{tag}",
                         [f"Xp{s}{tag}"])
                gap()
            pace[0] = "post_gap"
            per_head("Vnp", cut(XT), cut(V), [f"XT64{t[0]}" for t in parts])
            then("act", lambda e, b: e.copy(Vn[:], POST[:]), "Vn", ["Vnp"])
            gap()
            per_head("oT2p", cut(Vn), cut(IT), ["Vn"])
            then("act", lambda e, b: e.copy(oT2[:], POST[:]), "oT2", ["oT2p"])
            gap()
            project("x2p", oT2, wr, ["oT2"])
            then("dve", lambda e, b: e.tensor_tensor(x2, POST[:], x12[:], ALU.add), "x2",
                 ["x2p", "x12", ("x2out", 1), ("scat", 1)])
            st.dma("sp", lambda e, b: e.dma_start(T["out"][bass.ds(b, 1)].rearrange("o p d -> p (o d)"), x2),
                   "x2out", L_x2, after=["x2"])
            norm(x2, xn3, st3, mv3, rs3, "3", "x2", [])
            pace[0] = "route_gap"
            pe(lambda e, b: transposes(e, POST, cut(xn3)), "xn3Tp", ["xn3"])
            then("act", lambda e, b: e.copy(xn3T[:], POST[:]), "xn3T", ["xn3Tp"])
            gap()

            def logits(e, b):
                for c in range(DC):
                    i = e.matmul(POST[:, 0:E], xn3T[:, c * P:(c + 1) * P], wg[:, c, :], start=c == 0,
                                 stop=c == DC - 1)
                return i
            pe(logits, "lgp", ["xn3T"])
            then("dve", lambda e, b: e.tensor_copy(lg[:], POST[:, 0:E]), "lg0", ["lgp"])
            then("dve", lambda e, b: e.tensor_reduce(sc[:, 0:1], lg[:], AX.X, ALU.max, negate=True), "lmax",
                 ["lg0", ("eg", 1)])
            then("act", lambda e, b: e.activation(eg[:], lg[:], ACT.Exp, bias=sc[:, 0:1],
                                                  accum_out=sc[:, 1:2]), "eg", ["lmax", ("gate", 1)])
            then("dve", lambda e, b: e.tensor_reduce(sc[:, 2:3], eg[:], AX.X, ALU.max), "emax", ["eg"])
            then("dve", lambda e, b: e.scalar_tensor_tensor(oh2[:], eg[:], sc[:, 2:3], iota[:], ALU.is_ge, ALU.mult),
                 "cand", ["emax"])
            then("dve", lambda e, b: e.tensor_reduce(sc[:, 3:4], oh2[:], AX.X, ALU.min), "best", ["cand"])
            then("dve", lambda e, b: e.tensor_scalar(oh[:], iota[:], sc[:, 3:4], None, ALU.is_equal), "oh",
                 ["best"])
            gap(0.6)

            def places(e, b):
                e.matmul(POST[:, 0:E], cst[:, C_UPPER, :], oh[:], start=True, stop=False)
                return e.matmul(POST[:, 0:E], cst[:, C_ONES, :], before[:], start=False, stop=True)
            pe(places, "locp", ["oh", "lg0", ("before", 1)])
            then("dve", lambda e, b: e.tensor_tensor(oh2[:], POST[:, 0:E], oh[:], ALU.mult), "lg", ["locp"])
            then("dve", lambda e, b: e.tensor_tensor(before[:], before[:], oh[:], ALU.add), "before", ["locp"])
            then("dve", lambda e, b: e.tensor_reduce(sc[:, 4:5], oh2[:], AX.X, ALU.add), "loc", ["lg"])
            then("dve", lambda e, b: e.tensor_scalar(sc[:, 5:6], sc[:, 4:5], float(CAP), None, ALU.is_lt), "valid",
                 ["loc"])
            then("dve", lambda e, b: e.tensor_scalar(sc[:, 6:7], sc[:, 4:5], float(CAP - 1), None, ALU.min), "locc",
                 ["loc"])
            then("dve", lambda e, b: e.tensor_scalar(sc[:, 7:8], sc[:, 3:4], float(CAP), float(E * CAP), ALU.mult,
                                                     ALU.add), "row0", ["best"])
            then("dve", lambda e, b: e.tensor_tensor(sc[:, 8:9], sc[:, 7:8], sc[:, 6:7], ALU.add), "row",
                 ["row0", "locc"])
            then("dve", lambda e, b: e.tensor_tensor(sc[:, 9:10], sc[:, 8:9], cst[:, C_DUMP, 0:1], ALU.subtract),
                 "d0", ["row"])
            then("dve", lambda e, b: e.scalar_tensor_tensor(sc[:, 10:11], sc[:, 9:10], sc[:, 5:6],
                                                            cst[:, C_DUMP, 0:1], ALU.mult, ALU.add), "d1",
                 ["d0", "valid"])
            then("dve", lambda e, b: e.tensor_copy(sidx[:], sc[:, 10:11]), "sidx", ["d1", ("scat", 1)])
            then("dve", lambda e, b: e.reciprocal(route[:, 2 * D:2 * D + 1], sc[:, 1:2]), "gate", ["eg"])
            then("dve", lambda e, b: e.tensor_copy(route[:, 2 * D + 1:ROUTE].bitcast(U32), token[:]), "token",
                 [("token1", 1)])
            then("dve", lambda e, b: e.tensor_scalar(token[:], token[:], float(P), None, ALU.add), "token1",
                 ["token"])
            st.dma("pool", lambda e, b: scatter(e), "scat", L_scat, after=["sidx", "xn3", "gate", "token"])

        pre, att_st, tail, post = {}, {}, {}, {}
        all_lanes = list(lanes.values()) + L_ctx + [L_x, L_xr, L_x2, L_scat] + L_mrow
        for q in (0, 1):
            names = ev if q == 0 else {}
            keep_n = [l.n for l in all_lanes]
            if q:
                for l in [l for l in all_lanes if l not in L_ctx + [L_x]]:
                    l.n = 0
            pre[q], post[q] = Stage("prep", lanes, names), Stage("post", lanes, names)
            prep_steps(pre[q], q, [T_BANK])
            am, mx, tail[q] = (Stage(n, lanes, names) for n in ("attn", "max", "tail"))
            attn_steps(am, tail[q], q)
            att_st[q] = [am, mx]
            for g in range(1, HG):
                maxima(mx, g, q, 16.0 * (g - 1) + AT["max"], AT["max_pace"])
            post_steps(post[q], q, [POST])
            post[q].stretch(AT["post_end"])
            if q:
                assert keep_n == [l.n for l in all_lanes]
        for l in all_lanes:
            l.per, l.n = l.n, 0
        pre_first = Stage("prep", lanes, {})
        prep_steps(pre_first, 0, [T_BANK, *B_BANK, PV_BANK])
        assert all(l.n in (0, l.per) for l in all_lanes)
        for l in all_lanes:
            l.n = 0
        ev_last = {}
        post_last = Stage("post", lanes, ev_last)
        post_steps(post_last, (B - 1) % 2, [POST, KV_BANK, T_BANK, PV_BANK])
        last_n = {l: l.n or l.per for l in all_lanes}

        def parts(i, known):
            out = []
            for off, sts in ((2, lambda q: [load]), (1, lambda q: [pre[q]]), (0, lambda q: att_st[q]),
                             (-1, lambda q: [tail[q], post[q]])):
                if known is not None:
                    b = known + off
                    if not 0 <= b < B:
                        continue
                    other = {pre[0]: pre_first} if b == 0 else {post[b % 2]: post_last} if b == B - 1 else {}
                    out += [(other.get(s, s), b) for s in sts(b % 2)]
                else:
                    reg, d = i
                    out += [(s, (reg, d + off)) for s in sts((d + off) % 2)]
            return out

        s_first, s_w, s_c, s_setup, s_zero, s_wq, s_sp = (ctx.enter_context(nc.semaphore(n)) for n in (
            "first_in", "w_in", "const_in", "setup_dve", "zero_out", "wq_in", "setup_pool"))
        SETUP = 7

        def run(e, eng):
            for i in (-2, -1, 0, 1):
                if i == -1 and eng == "pe":
                    e.wait_ge(s_wq, 16)
                if i == 0 and eng in ("act", "dve"):
                    e.wait_ge(s_c, 16 * 5)
                if i == 1:
                    e.wait_ge(s_w, 16 * 5)
                    e.wait_ge(s_c, 16 * 5)
                    for l in decay_lanes.values():
                        e.wait_ge(l.sem, l.n)
                    e.wait_ge(s_zero, 16 * (ROWS // P + 1))
                issue(e, eng, parts(None, i) + ([(clear, 0), (decays, 0)] if i == 0 else []), ev)
            with e.Fori(2, B - 3, 2) as r:
                bases = {}
                for d in (0, 1):
                    issue(e, eng, parts((r, d), None), ev, bases)
            for i in (B - 2, B - 1, B):
                issue(e, eng, parts(None, i), ev, now=ev_last if i == B else {})
                if i == B - 2 and eng == "sp":
                    lane, k = ev[f"T{KB - 1}"]
                    e.wait_ge(lane.sem, (B - 1) * lane.per + k)
                    for j in (0, 1):
                        load_w1(e, T, w1_first, 0, j).then_inc(w1_sems[j], 16)

        block = ctx.enter_context(nc.Block())

        def weight(e, dst, src, sem):
            return e.dma_start(dst, T[src].rearrange("(c p) n -> p c n", p=P)).then_inc(sem, 16)

        clear = Stage("clear", lanes, ev)
        clear.at(1.0)
        for dst, src in ((wo, "Wo"), (ww, "WwT"), (wr, "WrT"), (wg, "Wg")):
            clear.step("act", lambda e, b, dst=dst, src=src: weight(e, dst[:], src, s_w))
        clear.step("act", lambda e, b: e.dma_start(bo[:], T["bo"]).then_inc(s_w, 16))
        for n in range(ROWS // P + 1):
            clear.at(3.0 * n + 2.0)
            clear.step("act", lambda e, b, n=n: e.dma_start(T["disp"][n * P:(n + 1) * P, :], route[:]).then_inc(
                s_zero, 16))

        decay_lanes = {("decays", e): lane(f"decays_{e}") for e in ("act", "dve")}
        decays = Stage("decays", decay_lanes, ev)
        decays.at(20.0)
        decays.step("act", lambda e, b: e.activation(logg[:], decay[:], ACT.Exp, scale=-1.0), "g_exp")
        decays.step("act", lambda e, b: e.activation(alpha[:], lalpha[:], ACT.Exp), "alpha")
        decays.step("dve", lambda e, b: e.tensor_scalar(logg[:], logg[:], 1.0, None, ALU.add), "g_add", ["g_exp"])
        decays.step("dve", lambda e, b: e.reciprocal(logg[:], logg[:]), "gamma", ["g_add"])
        decays.at(21.5)
        decays.step("act", lambda e, b: e.activation(logg[:], logg[:], ACT.Ln), "logg", ["gamma"])
        decays.step("dve", lambda e, b: e.tensor_scalar(token[:], cst[:, C_DUMP, 0:1], float(-ROWS), None, ALU.add),
                    "token_first")
        for h in range(DH):
            decays.at(23.0 + 2 * h)
            decays.step("act", lambda e, b, h=h: e.activation(decT[:, h, :], expo[:, 0, :], ACT.Exp,
                                                              scale=logg[:, h:h + 1]), f"decT{h}", ["logg"])
            decays.step("act", lambda e, b, h=h: e.activation(decI[:, h, :], expo[:, 1, :], ACT.Exp,
                                                              scale=logg[:, h:h + 1]), f"decI{h}", ["logg"])
            decays.at(24.0 + 2 * h)
            decays.step("dve", lambda e, b, h=h: e.tensor_tensor(decT[:, h, :], decT[:, h, :], cst[:, C_UPPER, :],
                                                                 ALU.mult), f"decT_cut{h}", [f"decT{h}"])
            decays.step("dve", lambda e, b, h=h: e.scalar_tensor_tensor(
                decI[:, h, :], decI[:, h, :], alpha[:, h:h + 1], cst[:, C_UPPER, :], ALU.mult, ALU.mult),
                f"decI_cut{h}", [f"decI{h}", "alpha"])
        for l in decay_lanes.values():
            l.per = l.n

        @block.sync
        def _(e):
            weight(e, wkv[:, :, 0:HD], "Wk", s_first)
            weight(e, wkv[:, :, HD:2 * HD], "Wv", s_first)
            for dst, src in ((ident, T["consts"][:, C_IDENT, :]), (bq[:], T["bq"]), (bkv[0:HD, :], T["bk"]),
                             (bkv[HD:2 * HD, :], T["bv"])):
                e.dma_start(dst, src).then_inc(s_first, 16)
            run(e, "sp")
            for l in all_lanes:
                if l.per:
                    e.wait_ge(l.sem, (B - 1) * l.per + last_n[l])

        @block.gpsimd
        def _(e):
            e.memset(route[:, 0:ROUTE - 1], 0.0).then_inc(s_sp, 1)
            e.memset(route[:, ROUTE - 1:ROUTE], 1.0).then_inc(s_sp, 1)
            e.memset(mhalf[:], -0.5).then_inc(s_sp, 1)
            e.memset(eps[:], EPS).then_inc(s_sp, 1)
            e.memset(before[:], 0.0).then_inc(s_sp, 1)
            e.memset(rkT[:, :, 0:1], 0.0).then_inc(s_sp, 1)
            e.wait_ge(s_sp, 6)
            e.memset(kvs[2 * HD:P, :], 0.0).then_inc(s_sp, 1)
            e.wait_ge(s_sp, 7)
            run(e, "pool")

        @block.scalar
        def _(e):
            weight(e, wq[:], "Wq", s_wq)
            for dst, src in ((cst[:, C_UPPER:NCONST, :], T["consts"][:, C_UPPER:NCONST, :]),
                             (expo, T["consts"][:, C_EXPO:C_EXPO + 2, :]), (iota[:], T["iota"]),
                             (decay[:], T["decay"]), (lalpha[:], T["log_alpha"])):
                e.dma_start(dst, src).then_inc(s_c, 16)
            e.wait_ge(s_sp, 7)
            run(e, "act")

        @block.vector
        def _(e):
            n = [0]

            def own(ins):
                n[0] += 1
                ins.then_inc(s_setup, 1)
                e.wait_ge(s_setup, n[0])
            for q in (0, 1):
                own(e.memset(v3[q][:, :, 2 * HD:2 * HD + 1].bitcast(F32), 1.0))
            for q in (0, 1):
                own(e.memset(kT[q][3 * HD:3 * HD + 1, :].bitcast(F32), 1.0))
            e.wait_ge(s_first, 16 * 6)
            own(e.tensor_scalar(bq[:], bq[:], SCALE, None, ALU.mult))
            own(e.tensor_copy(wkv2[:, :, 0:2 * HD], wkv))
            own(e.tensor_tensor(wkv2[:, :, 2 * HD:4 * HD], wkv, wkv2[:, :, 0:2 * HD].bitcast(F32), ALU.subtract))
            assert n[0] == SETUP
            e.wait_ge(s_sp, 7)
            run(e, "dve")

        @block.tensor
        def _(e):
            e.wait_ge(s_setup, SETUP)
            e.wait_ge(s_sp, 7)
            run(e, "pe")


def second_pipeline(nc, T, w1_first, w1_sems):
    with ExitStack() as ctx:
        def sb(name, shape, dt=F32):
            return ctx.enter_context(nc.sbuf_tensor(name, shape, dt))

        def lane(name):
            return Lane(ctx.enter_context(nc.semaphore(name)))

        bank = [ctx.enter_context(nc.psum_tensor(f"ebank{i}", [P, 512], F32)) for i in range(8)]
        T_BANK, H_BANK, Y_BANK = bank[0], bank[1:5], bank[5:7]
        w1 = [w1_first, sb("w11", [P, DC, F])]
        w2 = [sb(f"w2{i}", [P, FT, D]) for i in range(2)]
        dis = [sb(f"dis{i}", [P, ROUTE]) for i in range(2)]
        index = [sb(f"index{i}", [P, 1], U32) for i in range(2)]
        pad = sb("pad", [P, 2])
        dT = [sb(f"dT{i}", [P, DC, P]) for i in range(2)]
        hh = [sb(f"hh{i}", [P, 4 * P], F32R) for i in range(2)]
        hl = [sb(f"hl{i}", [P, 4 * P], F32R) for i in range(2)]
        w2h, w2l = ([sb(f"{n}{i}", [P, 4, D], F32R) for i in range(m)] for n, m in (("w2h", 4), ("w2l", 2)))
        eo = [sb(f"eo{i}", [P, D]) for i in range(2)]
        ident = sb("eident", [P, P])
        lanes = {(s, e): lane(f"{s}_{e}") for s, e in (
            ("turn", "pe"), ("turn", "dve"), ("split", "act"), ("split", "dve"), ("split", "pool"),
            ("expert", "pe"), ("expert", "dve"), ("expert", "act"), ("expert", "pool"))}
        L_w1 = [[Lane(s) for s in w1_sems], [lane(f"w1_in1{j}") for j in range(2)]]
        L_w2 = [[lane(f"w2_in{i}{j}") for j in range(2)] for i in range(2)]
        L_d, L_y = [lane(f"rows_in{i}") for i in range(2)], [lane(f"rows_out{i}") for i in range(2)]
        s_pad = ctx.enter_context(nc.semaphore("pad_set"))
        s_id = ctx.enter_context(nc.semaphore("ident_in"))
        ev, load, turn, comp = {}, {}, {}, {}
        for q in (0, 1):
            names = ev
            ld = Stage("load", lanes, names)
            mine = names if q == 0 else {}
            cp, tn, sp = Stage("expert", lanes, mine), Stage("turn", lanes, mine), Stage("split", lanes, mine)
            if q:
                for l in lanes.values():
                    l.per, l.n = l.n, 0
            ld.at(0.0)
            ld.dma("sp", lambda e, b, q=q: e.dma_start(dis[q][:], T["disp"].rearrange("(n p) d -> n p d", p=P)[
                bass.ds(b, 1)].rearrange("o p d -> p (o d)")), f"rows{q}", L_d[q], after=[("eo", 2)])
            for j in range(2):
                ld.at(1.0 + j)
                ld.dma("sp", lambda e, b, q=q, j=j: load_w1(e, T, w1[q], b, j), f"w1{q}{j}", L_w1[q][j],
                    after=[(f"H{2 * j + 1}", 2)])
            for j in range(2):
                ld.at(3.0 + j)
                ld.dma("sp", lambda e, b, q=q, j=j: e.dma_start(
                    w2[q][:, 8 * j:8 * j + 8, :], T["w2"][bass.ds(b, 1)].rearrange(
                        "o (h c p) m -> h p (o c) m", p=P, h=2)[j]), f"w2{q}{j}", L_w2[q][j],
                    after=[(f"Y{2 * j + 1}", 2)])

            def turn_rows(e, b, q=q):
                for c in range(DC):
                    i = e.transpose(T_BANK[:, c * P:(c + 1) * P], dis[q][:, c * P:(c + 1) * P], ident[:])
                return i
            tn.at(AT["rows_turn"])
            tn.step("pe", turn_rows, "dTp", [f"rows{q}", ("dT", 1)])
            tn.step("dve", lambda e, b, q=q: e.tensor_copy(dT[q][:].rearrange("p c t -> p (c t)"), T_BANK[:]), "dT",
                    ["dTp", ("H3", 2)])

            for g in range(4):
                sp.at(AT["w2_split"] + g)
                sp.step("act", lambda e, b, q=q, g=g: e.copy(w2h[g][:], w2[q][:, 4 * g:4 * g + 4, :]), f"w2h{g}",
                        [f"w2{q}{g // 2}", (f"Y{g}", 1)])
                for half, on in enumerate(("dve", "pool")):
                    to = slice(2 * half, 2 * half + 2)
                    sp.step(on, lambda e, b, q=q, g=g, to=to, half=half: e.tensor_tensor(
                        w2l[g % 2][:, to, :], w2[q][:, 4 * g + 2 * half:4 * g + 2 * half + 2, :],
                        w2h[g][:, to, :].bitcast(F32), ALU.subtract), f"w2l{g}{half}",
                        [f"w2h{g}", f"Y{g - 2}" if g > 1 else (f"Y{g + 2}", 1)])

            def up(e, b, g, q):
                for f in range(4):
                    for c in range(DC):
                        i = e.matmul(H_BANK[g][:, f * P:(f + 1) * P],
                                     w1[q][:, c, (4 * g + f) * P:(4 * g + f + 1) * P], dT[q][:, c, :],
                                     start=c == 0, stop=c == DC - 1)
                return i

            def down(e, b, g, q):
                for f in range(4):
                    part, k = slice(f * P, (f + 1) * P), 4 * g + f
                    e.matmul(Y_BANK[q][:], hh[g % 2][:, part], w2h[g][:, f, :], start=k == 0, stop=False)
                    e.matmul(Y_BANK[q][:], hh[g % 2][:, part], w2l[g % 2][:, f, :], start=False, stop=False)
                    i = e.matmul(Y_BANK[q][:], hl[g % 2][:, part], w2h[g][:, f, :], start=False, stop=k == FT - 1)
                return i

            def weigh(g, cp=cp, down=down, q=q):
                cp.step("pe", lambda e, b: down(e, b, g, q), f"Y{g}",
                        [f"hl{g}", f"w2l{g}0", f"w2l{g}1"] + ([("eo", 2)] if g == 0 else []))

            for g in range(4):
                cp.at(1.0 + g)
                cp.step("pe", lambda e, b, g=g, q=q: up(e, b, g, q), f"H{g}",
                        [f"w1{q}{g // 2}", "dT", (f"hl{g}", 1)])
                if g:
                    weigh(g - 1)
                cp.at(1.0 + g + AT["relu"])
                cp.step("act", lambda e, b, g=g: e.activation(hh[g % 2][:], H_BANK[g][:], ACT.Relu), f"hh{g}",
                        [f"H{g}", f"Y{g - 2}" if g > 1 else (f"Y{g + 2}", 1)])
                cp.step("dve", lambda e, b, g=g: e.scalar_tensor_tensor(
                    hl[g % 2][:], H_BANK[g][:], 0.0, hh[g % 2][:].bitcast(F32), ALU.max, ALU.subtract), f"hl{g}",
                    [f"hh{g}"])
            cp.at(5.0)
            weigh(3)
            cp.step("dve", lambda e, b, q=q: e.tensor_copy(index[q][:], dis[q][:, ROUTE - 1:ROUTE].bitcast(U32)),
                    "index", [f"rows{q}", (f"out{q}", 2)])
            cp.step("dve", lambda e, b, q=q: e.scalar_tensor_tensor(
                eo[q][:], Y_BANK[q][:], dis[q][:, 2 * D:2 * D + 1], dis[q][:, D:2 * D], ALU.mult, ALU.add), "eo",
                ["Y3", (f"out{q}", 2)])

            cp.step("pool", lambda e, b: e.tensor_tensor(pad[:, 0:1], pad[:, 1:2], pad[:, 1:2], ALU.mult), "hold",
                    ["eo", "index", ("hold", 1)])

            def scatter(e, q=q):
                return e.indirect_dma_start(
                    out=T["out"].rearrange("b p d -> (b p) d"),
                    out_offset=bass.IndirectOffsetOnAxis(ap=index[q][:, 0:1], axis=0), in_=eo[q][:],
                    in_offset=None, bounds_check=B * P - 1, oob_is_err=False)
            cp.dma("pool", lambda e, b, f=scatter: f(e), f"out{q}", L_y[q])
            for n, v in mine.items():
                ev.setdefault(n, v)
            load[q], turn[q], comp[q] = [ld], [tn], [cp, sp]
        for (_, l) in lanes.items():
            assert l.per == l.n
        halves = L_d + L_y + [l for x in L_w1 + L_w2 for l in x]
        for l in halves:
            l.per = 8
        for n, (l, k) in list(ev.items()):
            if l in halves:
                ev[n] = (l, 16 - 8 * int(n[-1 if l in L_d + L_y else -2]))

        def run(e, eng):
            def parts(r, i):
                b = [(load, i + 1), (turn, i + 1), (comp, i)]
                if r is None:
                    return [(s, n) for st, n in b if 0 <= n < E for s in st[n % 2]]
                return [(s, (r, n)) for st, n in b for s in st[n % 2]]
            late = Stage("load", lanes, ev)
            late.steps = [s for s in load[0][0].steps if s[3][0] not in L_w1[0]]
            issue(e, eng, [(late, 0), (turn[0][0], 0)], ev)
            for i in (0, 1):
                issue(e, eng, parts(None, i), ev)
            with e.Fori(2, E - 3, 2) as r:
                bases = {}
                for d in (0, 1):
                    issue(e, eng, parts(r, d), ev, bases)
            for i in (E - 2, E - 1):
                issue(e, eng, parts(None, i), ev)

        block = ctx.enter_context(nc.Block())

        @block.sync
        def _(e):
            e.dma_start(ident[:], T["consts"][:, C_IDENT, :]).then_inc(s_id, 16)
            run(e, "sp")
            for l in list(lanes.values()) + halves:
                if l.per:
                    e.wait_ge(l.sem, E * l.per)

        @block.tensor
        def _(e):
            e.wait_ge(s_id, 16)
            run(e, "pe")

        @block.gpsimd
        def _(e):
            e.memset(pad[:], 0.0).then_inc(s_pad, 1)
            e.wait_ge(s_pad, 1)
            run(e, "pool")

        @block.scalar
        def _(e):
            run(e, "act")

        @block.vector
        def _(e):
            run(e, "dve")


def program(nc, T):
    with ExitStack() as ctx:
        w1_first = ctx.enter_context(nc.sbuf_tensor("w1_first", [P, DC, F], F32))
        w1_sems = [ctx.enter_context(nc.semaphore(f"w1_in0{j}")) for j in range(2)]
        first_pipeline(nc, T, w1_first, w1_sems)
        second_pipeline(nc, T, w1_first, w1_sems)


def tables():
    c = np.zeros((P, NCONST + 2, P), np.float32)
    r, q = np.arange(P)[:, None], np.arange(P)[None, :]
    c[:, C_IDENT] = r == q
    same = r // CH == q // CH
    c[:, C_EXPO] = np.where(r < q, np.where(same, q - r, CH - 1 - r), 0)
    c[:, C_EXPO_I] = np.where(r < q, np.where(same, q - r, q - 1 - r), 0)
    c[:, C_UPPER] = r < q
    c[:, C_PAIR] = -1.0 * ((q % 2 == 1) & (r == q - 1))
    c[:, C_ONES] = 1.0
    c[:, C_DUMP] = ROWS + r
    for n in range(6):
        s = 2 << n
        c[:, C_LEVEL + n] = (r // (2 * s) == q // (2 * s)) & (r % (2 * s) >= s) & (q % (2 * s) < s)
    return c


def kernel(**inputs):
    from concourse import bacc
    from concourse.bass_utils import run_bass_kernel_spmd

    nc = bacc.Bacc("TRN2", target_bir_lowering=False, num_devices=1)
    g = {k: np.asarray(v) for k, v in inputs.items()}

    def rows(v):
        return np.ascontiguousarray(np.broadcast_to(v[None, :], (P, v.shape[0])))
    arrays = {
        "x": g["x"], "ctx": g["ctx_1024"], "Wq": g["L0_xattn_Wq"], "Wk": g["L0_xattn_Wk"],
        "Wv": g["L0_xattn_Wv"], "Wo": g["L0_xattn_Wo"], "bq": rows(g["L0_xattn_bq"]),
        "bk": g["L0_xattn_bk"].reshape(HD, 1), "bv": g["L0_xattn_bv"].reshape(HD, 1), "bo": rows(g["L0_xattn_bo"]),
        "WwT": np.ascontiguousarray(g["L0_attn_Ww"].T), "WrT": np.ascontiguousarray(g["L0_attn_Wr"].T),
        "decay": rows(g["L0_attn_decay"]), "log_alpha": rows(g["L0_attn_log_alpha"]), "Wg": g["L0_ffn_Wg"],
        "w1": g["L0_ffn_w1"], "w2": g["L0_ffn_w2"], "consts": tables(),
        "iota": rows(np.arange(E, dtype=np.float32) - E),
    }
    T = {k: nc.dram_tensor(f"in_{k}", v.shape, F32, kind="ExternalInput").ap() for k, v in arrays.items()}
    T["out"] = nc.dram_tensor("out", (B, P, D), F32, kind="ExternalOutput").ap()
    T["disp"] = nc.dram_tensor("dispatched", (ROWS + P, ROUTE), F32, kind="Internal").ap()
    program(nc, T)
    r = run_bass_kernel_spmd(nc, [{f"in_{k}": v for k, v in arrays.items()}], core_ids=[0])
    return r.results[0]["out"]
```
